# Optimizing a Trainium2 kernel written in Bass

```python
import numpy as np
import jax
import jax.numpy as jnp

def _softmax(x, axis=-1):
    return jax.nn.softmax(x, axis=axis)

def _gelu(x):
    return jax.nn.gelu(x, approximate=True)

def _silu(x):
    return jax.nn.silu(x)

def _sigmoid(x):
    return jax.nn.sigmoid(x)

def _layernorm(x, axis=-1, eps=1e-05):
    m = jnp.mean(x, axis=axis, keepdims=True)
    v = jnp.var(x, axis=axis, keepdims=True)
    return (x - m) / jnp.sqrt(v + eps)

def _scatter_add(tgt, idx, src, axis=0):
    return tgt.at[idx].add(src)

def _segment_sum(src, seg, n):
    return jax.ops.segment_sum(src, seg, n)
kernel_name = 'mk_adj_preln_d4_adj_r2_3ebd68'

def setup_inputs(seed: int=0):
    np.random.seed(seed)
    _w = jnp.asarray

    def _rec_inputs():
        import jax
        import jax.numpy as jnp
        _gk = jax.random.key(seed)
        x = -0.0002928 + 1 * jax.random.normal(jax.random.fold_in(_gk, 1), (128, 64, 256), jnp.float32)
        _a = jax.random.bernoulli(jax.random.fold_in(_gk, 2), 0.0625, (64, 64))
        _a = jnp.logical_or(_a, jnp.swapaxes(_a, -1, -2))
        _a = jnp.logical_or(_a, jnp.eye(64, dtype=bool))
        _af = _a.astype(jnp.float32)
        adj = _af
        return (x, adj)
    x, adj = _rec_inputs()

    def _L0_gnn_setup():
        import jax, jax.numpy as jnp
        import numpy as np
        B, N, D, H = (4, 1024, 256, 8)
        HD = D // H
        key = jax.random.key(seed)
        ks = jax.random.split(key, 10)
        x = jax.random.normal(ks[0], (B, N, D), dtype=jnp.float32)
        adj = (jax.random.uniform(ks[1], (N, N)) < 0.1).astype(jnp.float32)
        s = 1.0 / np.sqrt(D)
        Wq = jax.random.normal(ks[2], (D, D), dtype=jnp.float32) * s
        Wk = jax.random.normal(ks[3], (D, D), dtype=jnp.float32) * s
        Wv = jax.random.normal(ks[4], (D, D), dtype=jnp.float32) * s
        Wo = jax.random.normal(ks[5], (D, D), dtype=jnp.float32) * s
        bq = jnp.zeros((D,), jnp.float32)
        bk = jnp.zeros((D,), jnp.float32)
        bv = jnp.zeros((D,), jnp.float32)
        bo = jnp.zeros((D,), jnp.float32)
        return {'x': x, 'adj': adj, 'Wq': Wq, 'bq': bq, 'Wk': Wk, 'bk': bk, 'Wv': Wv, 'bv': bv, 'Wo': Wo, 'bo': bo}
    _L0_gnn_all = _L0_gnn_setup()
    _L0_gnn_in = {k: v for k, v in _L0_gnn_all.items() if k in ('Wq', 'bq', 'Wk', 'bk', 'Wv', 'bv', 'Wo', 'bo')}
    del _L0_gnn_all

    def _L1_gnn_setup():
        import jax, jax.numpy as jnp
        import numpy as np
        B, N, D, H = (16, 1025, 256, 8)
        LN_EPS = 1e-05

        def _make_mask(key, n):
            n_proto = n - 1
            adj = jax.random.bernoulli(key, 0.03, (n_proto, n_proto)).astype(jnp.float32)
            adj = jnp.clip(adj + adj.T + jnp.eye(n_proto, dtype=jnp.float32), 0.0, 1.0)
            mask = jnp.zeros((n, n), dtype=jnp.float32)
            mask = mask.at[0, :].set(1.0).at[:, 0].set(1.0)
            mask = mask.at[1:, 1:].set(adj)
            return mask
        key = jax.random.key(seed)
        ks = jax.random.split(key, 7)
        s = 1.0 / np.sqrt(D)
        return {'x': jax.random.normal(ks[0], (B, N, D), dtype=jnp.float32), 'w_qkv': jax.random.uniform(ks[1], (D, 3 * D), dtype=jnp.float32, minval=-s, maxval=s), 'w_proj': jax.random.uniform(ks[2], (D, D), dtype=jnp.float32, minval=-s, maxval=s), 'b_proj': jnp.zeros((D,), dtype=jnp.float32), 'ln_gamma': jnp.ones((D,), dtype=jnp.float32), 'ln_beta': jnp.zeros((D,), dtype=jnp.float32), 'attn_mask': _make_mask(ks[3], N)}
    _L1_gnn_all = _L1_gnn_setup()
    _L1_gnn_in = {k: v for k, v in _L1_gnn_all.items() if k in ('w_qkv', 'w_proj', 'b_proj', 'ln_gamma', 'ln_beta')}
    del _L1_gnn_all

    def _L2_gnn_setup():
        import jax, jax.numpy as jnp
        import numpy as np
        ALPHA = 0.2
        key = jax.random.key(seed)
        k0, k1, k2, k3 = jax.random.split(key, 4)
        B, N, C, F = (64, 512, 256, 256)
        x = jax.random.normal(k0, (B, N, C), dtype=jnp.float32)
        W = jax.random.normal(k1, (C, F), dtype=jnp.float32) * (1.414 / np.sqrt(C + F))
        a = jax.random.normal(k2, (2 * F, 1), dtype=jnp.float32) * (1.414 / np.sqrt(2 * F + 1))
        beta = jnp.ones((1,), dtype=jnp.float32)
        mask = (jax.random.uniform(k3, (N, N)) < 0.3).astype(jnp.float32)
        return {'x': x, 'W': W, 'a': a, 'beta': beta, 'mask': mask}
    _L2_gnn_all = _L2_gnn_setup()
    _L2_gnn_in = {k: v for k, v in _L2_gnn_all.items() if k in ('W', 'a', 'beta')}
    del _L2_gnn_all

    def _L3_gnn_setup():
        import jax, jax.numpy as jnp
        import numpy as np
        B, N, D, T = (64, 128, 256, 3)

        def _lin(v, W, b):
            return jnp.einsum('...i,oi->...o', v, W) + b
        key = jax.random.key(seed)
        ks = jax.random.split(key, 12)
        s2 = 1.0 / np.sqrt(2 * D)
        s1 = 1.0 / np.sqrt(D)
        return {'x': jax.random.normal(ks[0], (B, N, D), jnp.float32), 'in_mat': jax.random.uniform(ks[1], (N, N), jnp.float32) / N, 'out_mat': jax.random.uniform(ks[2], (N, N), jnp.float32) / N, 'w3_w': jax.random.normal(ks[3], (D, 2 * D), jnp.float32) * s2, 'w3_b': jnp.zeros((D,), jnp.float32), 'u3_w': jax.random.normal(ks[4], (D, D), jnp.float32) * s1, 'u3_b': jnp.zeros((D,), jnp.float32), 'w4_w': jax.random.normal(ks[5], (D, 2 * D), jnp.float32) * s2, 'w4_b': jnp.zeros((D,), jnp.float32), 'w5_w': jax.random.normal(ks[6], (D, 2 * D), jnp.float32) * s2, 'w5_b': jnp.zeros((D,), jnp.float32), 'u5_w': jax.random.normal(ks[7], (D, D), jnp.float32) * s1, 'u5_b': jnp.zeros((D,), jnp.float32)}
    _L3_gnn_all = _L3_gnn_setup()
    _L3_gnn_in = {k: v for k, v in _L3_gnn_all.items() if k in ('w3_w', 'w3_b', 'u3_w', 'u3_b', 'w4_w', 'w4_b', 'w5_w', 'w5_b', 'u5_w', 'u5_b')}
    del _L3_gnn_all
    return {'x': x, 'adj': adj, 'L0_gnn_Wq': _L0_gnn_in['Wq'], 'L0_gnn_bq': _L0_gnn_in['bq'], 'L0_gnn_Wk': _L0_gnn_in['Wk'], 'L0_gnn_bk': _L0_gnn_in['bk'], 'L0_gnn_Wv': _L0_gnn_in['Wv'], 'L0_gnn_bv': _L0_gnn_in['bv'], 'L0_gnn_Wo': _L0_gnn_in['Wo'], 'L0_gnn_bo': _L0_gnn_in['bo'], 'L1_gnn_w_qkv': _L1_gnn_in['w_qkv'], 'L1_gnn_w_proj': _L1_gnn_in['w_proj'], 'L1_gnn_b_proj': _L1_gnn_in['b_proj'], 'L1_gnn_ln_gamma': _L1_gnn_in['ln_gamma'], 'L1_gnn_ln_beta': _L1_gnn_in['ln_beta'], 'L2_gnn_W': _L2_gnn_in['W'], 'L2_gnn_a': _L2_gnn_in['a'], 'L2_gnn_beta': _L2_gnn_in['beta'], 'L3_gnn_w3_w': _L3_gnn_in['w3_w'], 'L3_gnn_w3_b': _L3_gnn_in['w3_b'], 'L3_gnn_u3_w': _L3_gnn_in['u3_w'], 'L3_gnn_u3_b': _L3_gnn_in['u3_b'], 'L3_gnn_w4_w': _L3_gnn_in['w4_w'], 'L3_gnn_w4_b': _L3_gnn_in['w4_b'], 'L3_gnn_w5_w': _L3_gnn_in['w5_w'], 'L3_gnn_w5_b': _L3_gnn_in['w5_b'], 'L3_gnn_u5_w': _L3_gnn_in['u5_w'], 'L3_gnn_u5_b': _L3_gnn_in['u5_b']}

def reference(x, adj, L0_gnn_Wq, L0_gnn_bq, L0_gnn_Wk, L0_gnn_bk, L0_gnn_Wv, L0_gnn_bv, L0_gnn_Wo, L0_gnn_bo, L1_gnn_w_qkv, L1_gnn_w_proj, L1_gnn_b_proj, L1_gnn_ln_gamma, L1_gnn_ln_beta, L2_gnn_W, L2_gnn_a, L2_gnn_beta, L3_gnn_w3_w, L3_gnn_w3_b, L3_gnn_u3_w, L3_gnn_u3_b, L3_gnn_w4_w, L3_gnn_w4_b, L3_gnn_w5_w, L3_gnn_w5_b, L3_gnn_u5_w, L3_gnn_u5_b):
    import jax
    import jax.numpy as jnp

    def _L0_gnn_ref(x, adj, Wq, bq, Wk, bk, Wv, bv, Wo, bo):
        import jax, jax.numpy as jnp
        import numpy as np
        B, N, D, H = (4, 1024, 256, 8)
        HD = D // H
        b, n, d = x.shape
        q = (x @ Wq + bq).reshape(b, n, H, HD)
        k = (x @ Wk + bk).reshape(b, n, H, HD)
        v = (x @ Wv + bv).reshape(b, n, H, HD)
        scores = jnp.einsum('bqhd,bkhd->bhqk', q, k) / jnp.sqrt(jnp.float32(HD))
        scores = scores + (1.0 - adj)[None, None, :, :] * -1000000000.0
        attn = jax.nn.softmax(scores, axis=-1)
        out = jnp.einsum('bhqk,bkhd->bqhd', attn, v).reshape(b, n, d)
        return out @ Wo + bo

    def _L1_gnn_ref(x, w_qkv, w_proj, b_proj, ln_gamma, ln_beta, attn_mask):
        import jax, jax.numpy as jnp
        import numpy as np
        B, N, D, H = (16, 1025, 256, 8)
        LN_EPS = 1e-05

        def _make_mask(key, n):
            n_proto = n - 1
            adj = jax.random.bernoulli(key, 0.03, (n_proto, n_proto)).astype(jnp.float32)
            adj = jnp.clip(adj + adj.T + jnp.eye(n_proto, dtype=jnp.float32), 0.0, 1.0)
            mask = jnp.zeros((n, n), dtype=jnp.float32)
            mask = mask.at[0, :].set(1.0).at[:, 0].set(1.0)
            mask = mask.at[1:, 1:].set(adj)
            return mask
        b, n, d = x.shape
        hd = d // H
        scale = hd ** (-0.5)
        qkv = (x @ w_qkv).reshape(b, n, 3, H, hd).transpose(2, 0, 3, 1, 4)
        q, k, v = (qkv[0], qkv[1], qkv[2])
        attn = jnp.einsum('bhnd,bhmd->bhnm', q, k) * scale
        attn = jnp.where(attn_mask[None, None] == 0, -jnp.inf, attn)
        attn = jax.nn.softmax(attn, axis=-1)
        o = jnp.einsum('bhnm,bhmd->bhnd', attn, v).transpose(0, 2, 1, 3).reshape(b, n, d)
        o = o @ w_proj + b_proj
        mu = jnp.mean(o, axis=-1, keepdims=True)
        var = jnp.mean(jnp.square(o - mu), axis=-1, keepdims=True)
        ln = (o - mu) * jax.lax.rsqrt(var + LN_EPS) * ln_gamma + ln_beta
        return o + ln

    def _L2_gnn_ref(x, W, a, beta, mask):
        import jax, jax.numpy as jnp
        import numpy as np
        ALPHA = 0.2
        F_ = W.shape[1]
        h = jnp.einsum('bnc,cf->bnf', x, W)
        a1, a2 = (a[:F_, 0], a[F_:, 0])
        s1 = jnp.einsum('bnf,f->bn', h, a1)
        s2 = jnp.einsum('bnf,f->bn', h, a2)
        e = jax.nn.leaky_relu(s1[:, :, None] + s2[:, None, :], negative_slope=ALPHA)
        e = e * mask[None, :, :]
        att = jax.nn.softmax(e, axis=2)
        h_prime = jnp.einsum('bij,bjf->bif', att, h)
        return jax.nn.elu(h_prime + beta * h)

    def _L3_gnn_ref(x, in_mat, out_mat, w3_w, w3_b, u3_w, u3_b, w4_w, w4_b, w5_w, w5_b, u5_w, u5_b):
        import jax, jax.numpy as jnp
        import numpy as np
        B, N, D, T = (64, 128, 256, 3)

        def _lin(v, W, b):
            return jnp.einsum('...i,oi->...o', v, W) + b
        h = x
        for _ in range(T):
            a_in = jnp.einsum('nm,bmd->bnd', in_mat, h)
            a_out = jnp.einsum('nm,bmd->bnd', out_mat, h)
            av = jnp.concatenate([a_in, a_out], axis=-1)
            z = jax.nn.sigmoid(_lin(av, w3_w, w3_b) + _lin(h, u3_w, u3_b))
            r = jax.nn.sigmoid(_lin(av, w4_w, w4_b) + _lin(h, u3_w, u3_b))
            hv = jnp.tanh(_lin(av, w5_w, w5_b) + _lin(r * h, u5_w, u5_b))
            h = (1.0 - z) * h + z * hv
        return h
    h = jnp.maximum(_layernorm(x, axis=-1), 0.0)
    x = x + _L0_gnn_ref(h, adj, L0_gnn_Wq, L0_gnn_bq, L0_gnn_Wk, L0_gnn_bk, L0_gnn_Wv, L0_gnn_bv, L0_gnn_Wo, L0_gnn_bo)
    h = jnp.maximum(_layernorm(x, axis=-1), 0.0)
    x = x + _L1_gnn_ref(h, L1_gnn_w_qkv, L1_gnn_w_proj, L1_gnn_b_proj, L1_gnn_ln_gamma, L1_gnn_ln_beta, adj)
    h = jnp.maximum(_layernorm(x, axis=-1), 0.0)
    x = x + _L2_gnn_ref(h, L2_gnn_W, L2_gnn_a, L2_gnn_beta, adj)
    h = jnp.maximum(_layernorm(x, axis=-1), 0.0)
    x = x + _L3_gnn_ref(h, adj, adj, L3_gnn_w3_w, L3_gnn_w3_b, L3_gnn_u3_w, L3_gnn_u3_b, L3_gnn_w4_w, L3_gnn_w4_b, L3_gnn_w5_w, L3_gnn_w5_b, L3_gnn_u5_w, L3_gnn_u5_b)
    return x

_drawn_inputs = setup_inputs


def setup_inputs(seed=0):
    import zlib

    import numpy as np

    out = dict(_drawn_inputs(seed))
    spreads = {'L0_gnn_bq': (0.0, 0.778),
     'L0_gnn_bk': (0.0, 0.8),
     'L0_gnn_bv': (0.0, 0.1),
     'L0_gnn_bo': (0.0, 0.1),
     'L1_gnn_b_proj': (0.0, 0.1),
     'L1_gnn_ln_gamma': (1.0, 0.2),
     'L1_gnn_ln_beta': (0.0, 0.1),
     'L3_gnn_w3_b': (0.0, 0.356),
     'L3_gnn_u3_b': (0.0, 0.447),
     'L3_gnn_w4_b': (0.0, 0.8),
     'L3_gnn_w5_b': (0.0, 0.278),
     'L3_gnn_u5_b': (0.0, 0.1)}
    factors = {'L2_gnn_a': 7.924}
    for name, (base, spread) in spreads.items():
        noise = np.random.default_rng([zlib.crc32(name.encode()), seed]).standard_normal(out[name].shape)
        drawn = base * np.exp(spread * noise) if base else spread * noise
        out[name] = jnp.asarray(drawn.astype(out[name].dtype))
    for name, factor in factors.items():
        out[name] = (out[name] * factor).astype(out[name].dtype)
    return out
```

```python
import concourse.bass as bass
from concourse import mybir
from contextlib import ExitStack
import numpy as np

F32 = mybir.dt.float32
F32R = mybir.dt.float32r
ALU = mybir.AluOpType
ACT = mybir.ActivationFunctionType
AX = mybir.AxisListType

B, N, D = 128, 64, 256
HEADS = 8
HD = D // HEADS
P = 128
EPS = 1e-5
ALPHA = 0.2
TILES = B * N // P
CT = 4
CW = CT * P
CHUNKS = TILES // CT
FT = D // P
BANK = 512
STEPS = 3
MASKED = -3e38


def wait(eng, sem, count):
    if not isinstance(count, int) or count > 0:
        eng.wait_ge(sem, count)


def wait_apart(eng, sem, count):
    if not isinstance(count, int):
        eng.wait_ge(sem, 1)
    eng.wait_ge(sem, count)


def exists(chunk):
    return not isinstance(chunk, int) or 0 <= chunk < CHUNKS


class Phase(ExitStack):

    def __init__(self, nc):
        super().__init__()
        self.handles = []
        self.callback(self.clear, nc)

    def semaphore(self, nc, name):
        self.handles.append(nc.alloc_semaphore(name))
        return self.handles[-1]

    def clear(self, nc):
        nc.clear_and_free_semaphores(self.handles)
        nc.all_engine_barrier()


def f32(ap):
    return ap.bitcast(F32)


class Parts:

    def __init__(self, ctx, nc, name, shape):
        self.hi = ctx.enter_context(nc.sbuf_tensor(name + "_hi", shape, F32R))
        self.lo = ctx.enter_context(nc.sbuf_tensor(name + "_lo", shape, F32R))


def product(pe, out, stationary, moving, begins=True, ends=True):
    terms = []
    for s, m in zip(stationary, moving):
        terms += [(s[0], m[0]), (s[0], m[1]), (s[1], m[0])]
    for n, (s, m) in enumerate(terms):
        last = pe.matmul(out, s, m, start=(begins and n == 0),
                         stop=(ends and n == len(terms) - 1))
    return last


def pair(parts, *index):
    return parts.hi[index], parts.lo[index]


def spread_rows(ap, times):
    return ap.rearrange("(a n) -> a n", a=1).to_broadcast([times, ap.shape[0]])


def load_columns(ap):
    return ap.rearrange("(f p) -> p f", p=P)


class LayerNorm:

    def __init__(self, nc, ctx, tag, x, ident, transposed=True):
        def sb(name, shape, dt=F32):
            return ctx.enter_context(nc.sbuf_tensor(f"{tag}_{name}", shape, dt))

        def sem(name):
            return ctx.semaphore(nc, f"{tag}_{name}")

        self.x, self.ident = x, ident
        self.stats = sb("stats", [P, CT, 6])
        self.mean_var = sb("mean_var", [P, CT, 2])
        self.var_eps = sb("var_eps", [P, CT])
        self.rstd = sb("rstd", [P, CT])
        self.minus_half = sb("minus_half", [P, CT])
        self.eps = sb("eps", [P, CT])
        self.carrier = sb("carrier", [P, 1])
        self.xn = sb("xn", [P, CT, D])
        if transposed:
            self.hT = Parts(ctx, nc, f"{tag}_hT", [P, FT, CW])
        self.bn_done = sem("bn_done")
        self.stats_ready = sem("stats_ready")
        self.half_ready = sem("half_ready")
        self.var_ready = sem("var_ready")
        self.rstd_ready = sem("rstd_ready")
        self.xn_ready = sem("xn_ready")
        self.xT_ready = sem("xT_ready")
        self.hT_hi_ready = sem("hT_hi_ready")
        self.hT_lo_ready = sem("hT_lo_ready")

    def dve_carry(self, dve, sem, count):
        dve.wait_ge(sem, count)
        dve.memset(self.carrier[:], 0.0)

    def dve_stats(self, dve, c):
        for t in range(CT):
            last = dve.bn_stats(self.stats[:, t, :], self.x[:, bass.ds(c * CT + t, 1), :])
        last.then_inc(self.bn_done, 1)
        self.dve_carry(dve, self.bn_done, c + 1)
        for t in range(CT):
            last = dve.bn_aggr(self.mean_var[:, t, :], self.stats[:, t, :])
        last.then_inc(self.stats_ready, 1)

    def pool_setup(self, pool):
        pool.memset(self.minus_half[:], -0.5).then_inc(self.half_ready, 1)
        pool.memset(self.eps[:], EPS).then_inc(self.half_ready, 1)
        pool.wait_ge(self.half_ready, 2)

    def pool_rstd(self, pool, c):
        pool.wait_ge(self.stats_ready, c + 1)
        pool.tensor_tensor(self.var_eps[:], self.mean_var[:, :, 1], self.eps[:], ALU.add)\
            .then_inc(self.var_ready, 1)
        pool.wait_ge(self.var_ready, c + 1)
        pool.tensor_tensor(self.rstd[:], self.var_eps[:], self.minus_half[:], ALU.pow)\
            .then_inc(self.rstd_ready, 1)

    def dve_normalise(self, dve, c):
        dve.wait_ge(self.rstd_ready, c + 1)
        wait(dve, self.xT_ready, c * FT)
        for t in range(CT):
            last = dve.tensor_scalar(self.xn[:, t:t + 1, :], self.x[:, bass.ds(c * CT + t, 1), :],
                                     self.mean_var[:, t, 0:1], self.rstd[:, t:t + 1],
                                     ALU.subtract, ALU.mult)
        last.then_inc(self.xn_ready, 1)

    def pe_transpose(self, pe, c, f, bank):
        pe.wait_ge(self.xn_ready, c + 1)
        for t in range(CT):
            last = pe.transpose(bank[:, t * P:(t + 1) * P], self.xn[:, t, f * P:(f + 1) * P], self.ident[:])
        last.then_inc(self.xT_ready, 1)

    def act_high(self, act, c, f, bank):
        act.wait_ge(self.xT_ready, c * FT + f + 1)
        act.activation(self.hT.hi[:, f, :], bank, ACT.Relu).then_inc(self.hT_hi_ready, 1)

    def dve_low(self, dve, c, f, bank):
        dve.wait_ge(self.hT_hi_ready, c * FT + f + 1)
        dve.scalar_tensor_tensor(self.hT.lo[:, f, :], bank, 0.0, f32(self.hT.hi[:, f, :]),
                                 ALU.max, ALU.subtract).then_inc(self.hT_lo_ready, 1)


def attention_phase(nc, tag, x, ident, psum, w, first_load=None, tail_norm=None):
    scores, ring = psum
    R = P // HD
    SCALE = float(np.float32(1.0) / np.sqrt(np.float32(HD)))
    LAST = 2 if tail_norm else 1
    BEGIN = 3
    with Phase(nc) as ctx:
        def sb(name, shape, dt=F32):
            return ctx.enter_context(nc.sbuf_tensor(f"{tag}_{name}", shape, dt))

        def sem(name):
            return ctx.semaphore(nc, f"{tag}_{name}")

        ln = LayerNorm(nc, ctx, tag, x, ident)
        hT = ln.hT
        names = ["q", "k", "v", "o"]
        parts = {n: Parts(ctx, nc, f"{tag}_w{n}", [P, FT, D]) for n in names}
        stage = sb("stage", [P, len(names), FT, D])
        mask = sb("mask", [P, N])
        adj2 = sb("adj2", [P, N])
        mask1 = sb("mask1", [P, N])
        out_bias = sb("out_bias", [P, D])
        col_bias = sb("col_bias", [P, 3, FT])
        qT = sb("qT", [P, FT, CW])
        kT = sb("kT", [P, FT, CW])
        v = sb("v", [P, 2, CT, 2, P])
        s = sb("s", [P, 2, R, CT, 2, N])
        mx = sb("mx", [P, R, CT * 2])
        total = sb("total", [P, R, CT * 2])
        rtotal = sb("rtotal", [P, R, CT * 2])
        pT = sb("pT", [P, R, CT, P])
        oT = Parts(ctx, nc, f"{tag}_oT", [P, FT, CW])
        if tail_norm:
            o = sb("o", [P, CT, D])
            o_n = sb("o_n", [P, CT, D])
            o_stats = sb("o_stats", [P, CT, 6])
            o_mv = sb("o_mv", [P, CT, 2])
            o_var = sb("o_var", [P, CT])
            o_rstd = sb("o_rstd", [P, CT])
            gamma = sb("gamma", [P, D])
            beta = sb("beta", [P, D])

        w_loaded = [sem(f"w{n}_loaded") for n in names]
        small_loaded = sem("small_loaded")
        w_hi_ready = sem("w_hi_ready")
        w_lo_ready = sem("w_lo_ready")
        mask_steps = sem("mask_steps")
        qk_ready = sem("qk_ready")
        qk_copied = sem("qk_copied")
        v_ready = sem("v_ready")
        v_copied = sem("v_copied")
        s_ready = sem("s_ready")
        s_masked = sem("s_masked")
        s_max = sem("s_max")
        s_shifted = sem("s_shifted")
        p_exp = sem("p_exp")
        p_total = sem("p_total")
        p_rtotal = sem("p_rtotal")
        p_ready = sem("p_ready")
        pT_ready = sem("pT_ready")
        pT_copied = sem("pT_copied")
        oT_ready = sem("oT_ready")
        oT_hi_ready = sem("oT_hi_ready")
        oT_lo_ready = sem("oT_lo_ready")
        out_ready = sem("out_ready")
        x_biased = sem("x_biased")
        x_done = sem("x_done")
        if tail_norm:
            o_bn = sem("o_bn")
            o_mv_ready = sem("o_mv_ready")
            o_var_ready = sem("o_var_ready")
            o_rstd_ready = sem("o_rstd_ready")
            o_n_ready = sem("o_n_ready")
            o_scaled = sem("o_scaled")
            o_ln_ready = sem("o_ln_ready")
            x_plus_o = sem("x_plus_o")
            x_final = sem("x_final")

        x_loaded = [sem(f"x_loaded{n}") for n in range(3)] if first_load is not None else None
        X_CUTS = [0, 1, 3, CHUNKS]

        small = [(adj2[0:N, :], w["adj"]), (adj2[N:P, :], w["adj"]), (out_bias[:], spread_rows(w["bo"], P))]
        if "bq" in w:
            small += [(col_bias[:, n, :], load_columns(w[b])) for n, b in enumerate(("bq", "bk", "bv"))]
        if tail_norm:
            small += [(gamma[:], spread_rows(tail_norm["gamma"], P)), (beta[:], spread_rows(tail_norm["beta"], P))]

        def iterations(eng, body):
            for i in range(-1, BEGIN):
                body(i, i % 2)
            with eng.Fori(0, (CHUNKS - 3 - BEGIN) // 2) as j:
                body(j * 2 + BEGIN, 1)
                body(j * 2 + BEGIN + 1, 0)
            for i in range(CHUNKS - 3, CHUNKS + LAST):
                body(i, i % 2)

        with nc.Block() as block:
            @block.sync
            def _(sp):
                if first_load is not None:
                    xs = first_load.rearrange("b n d -> (b n) d").rearrange("(t p) d -> p t d", p=P)
                    sp.dma_start(x[:, 0:CT, :], xs[:, 0:CT, :]).then_inc(x_loaded[0], 16)
                for n, name in enumerate(names[:3]):
                    sp.dma_start(stage[:, n, :, :], w["w" + name]).then_inc(w_loaded[n], 16)
                for dst, src in small:
                    sp.dma_start(dst, src).then_inc(small_loaded, 16)
                sp.dma_start(stage[:, 3, :, :], w["wo"]).then_inc(w_loaded[3], 16)
                if first_load is not None:
                    for n in (1, 2):
                        a, b = X_CUTS[n] * CT, X_CUTS[n + 1] * CT
                        sp.dma_start(x[:, a:b, :], xs[:, a:b, :]).then_inc(x_loaded[n], 16)

            @block.gpsimd
            def _(pool):
                ln.pool_setup(pool)
                if tail_norm:
                    pool.wait_ge(small_loaded, 16 * len(small))
                else:
                    pool.wait_ge(small_loaded, 16 * len(small))

                def shift(i, par, r):
                    pool.wait_ge(s_max, i * R + r + 1)
                    sr = s[:, par, r, :, :, :].rearrange("p t m k -> p (t m) k")
                    pool.tensor_tensor(sr, sr, mx[:, r, :].unsqueeze(2).to_broadcast([P, CT * 2, N]),
                                       ALU.subtract).then_inc(s_shifted, 1)

                def normalise(i, par, r):
                    pool.wait_ge(p_rtotal, i * R + r + 1)
                    sr = s[:, par, r, :, :, :].rearrange("p t m k -> p (t m) k")
                    pool.tensor_tensor(sr, sr, rtotal[:, r, :].unsqueeze(2).to_broadcast([P, CT * 2, N]),
                                       ALU.mult).then_inc(p_ready, 1)

                def body(i, par):
                    if isinstance(i, int) and i == -1:
                        ln.pool_rstd(pool, 0)
                        ln.pool_rstd(pool, 1)
                        return
                    if exists(i + 2):
                        ln.pool_rstd(pool, i + 2)
                    if exists(i - 1) and not tail_norm:
                        c = i - 1
                        pool.wait_ge(ln.xn_ready, c + 1)
                        xc = x[:, bass.ds(c * CT, CT), :]
                        pool.tensor_tensor(xc, xc, out_bias[:].unsqueeze(1).to_broadcast([P, CT, D]),
                                           ALU.add).then_inc(x_biased, 1)
                    if tail_norm and exists(i - 2):
                        c = i - 2
                        pool.wait_ge(o_mv_ready, c + 1)
                        pool.tensor_tensor(o_var[:], o_mv[:, :, 1], ln.eps[:], ALU.add)\
                            .then_inc(o_var_ready, 1)
                        pool.wait_ge(o_var_ready, c + 1)
                        pool.tensor_tensor(o_rstd[:], o_var[:], ln.minus_half[:], ALU.pow)\
                            .then_inc(o_rstd_ready, 1)
                        xc = x[:, bass.ds(c * CT, CT), :]
                        pool.tensor_tensor(xc, xc, o[:], ALU.add).then_inc(x_plus_o, 1)
                    if exists(i):
                        shift(i, par, 0)
                        shift(i, par, 1)
                        shift(i, par, 2)
                        normalise(i, par, 0)
                        shift(i, par, 3)
                        for r in range(1, R):
                            normalise(i, par, r)
                    if tail_norm and exists(i - 2):
                        c = i - 2
                        pool.wait_ge(o_n_ready, c + 1)
                        pool.tensor_tensor(o_n[:], o_n[:], gamma[:].unsqueeze(1).to_broadcast([P, CT, D]),
                                           ALU.mult).then_inc(o_scaled, 1)
                        pool.wait_ge(o_scaled, c + 1)
                        pool.tensor_tensor(o_n[:], o_n[:], beta[:].unsqueeze(1).to_broadcast([P, CT, D]),
                                           ALU.add).then_inc(o_ln_ready, 1)

                iterations(pool, body)

            @block.scalar
            def _(act):
                for n in range(len(names)):
                    act.wait_ge(w_loaded[n], 16)
                    act.activation(parts[names[n]].hi[:], stage[:, n, :, :], ACT.Copy).then_inc(w_hi_ready, 1)
                if "bq" in w:
                    act.wait_ge(small_loaded, 16 * len(small))

                def body(i, par):
                    if exists(i):
                        for r in (0, 1):
                            act.wait_ge(s_shifted, i * R + r + 1)
                            sr = s[:, par, r, :, :, :]
                            act.activation(sr, sr, ACT.Exp).then_inc(p_exp, 1)
                    if exists(i - 1):
                        for r in range(R):
                            act.wait_ge(pT_ready, (i - 1) * R + r + 1)
                            act.activation(pT[:, r, :, :].rearrange("p t q -> p (t q)"), ring[:, r, :],
                                           ACT.Copy).then_inc(pT_copied, 1)
                    if exists(i + 1):
                        for f in range(FT):
                            ln.act_high(act, i + 1, f, ring[:, f, :])
                    if exists(i):
                        for r in (2, 3):
                            act.wait_ge(s_shifted, i * R + r + 1)
                            sr = s[:, par, r, :, :, :]
                            act.activation(sr, sr, ACT.Exp).then_inc(p_exp, 1)
                    if exists(i - 1):
                        for m in range(FT):
                            act.wait_ge(oT_ready, (i - 1) * FT + m + 1)
                            if "bq" in w:
                                ins = act.activation(oT.hi[:, m, :], ring[:, 2 + m, :], ACT.Identity,
                                                     bias=col_bias[:, 2, m:m + 1])
                            else:
                                ins = act.activation(oT.hi[:, m, :], ring[:, 2 + m, :], ACT.Copy)
                            ins.then_inc(oT_hi_ready, 1)
                    if exists(i + 1):
                        c = i + 1
                        for n, dst in enumerate((qT, kT)):
                            for m in range(FT):
                                act.wait_ge(qk_ready, c * 2 * FT + n * FT + m + 1)
                                if "bq" in w:
                                    ins = act.activation(dst[:, m, :], ring[:, 2 * n + m, :], ACT.Identity,
                                                         bias=col_bias[:, n, m:m + 1])
                                else:
                                    ins = act.activation(dst[:, m, :], ring[:, 2 * n + m, :], ACT.Copy)
                                ins.then_inc(qk_copied, 1)
                        for g in range(2):
                            act.wait_ge(v_ready, c * 2 + g + 1)
                            vb = ring[:, 2 + g, :].rearrange("p (t c) -> p t c", t=2)
                            for m in range(2):
                                for gr in range(2):
                                    last = act.activation(
                                        v[m * N:(m + 1) * N, 1 - par, 2 * g:2 * g + 2, gr, :],
                                        vb[gr * N:(gr + 1) * N, :, m * P:(m + 1) * P], ACT.Copy)
                            last.then_inc(v_copied, 1)

                iterations(act, body)

            @block.vector
            def _(dve):
                def chunk_loaded(c):
                    if first_load is not None and isinstance(c, int) and c in X_CUTS:
                        dve.wait_ge(x_loaded[X_CUTS.index(c)], 16)

                chunk_loaded(0)
                ln.dve_stats(dve, 0)
                for n in range(len(names)):
                    dve.wait_ge(w_hi_ready, n + 1)
                    dve.tensor_tensor(parts[names[n]].lo[:], stage[:, n, :, :], f32(parts[names[n]].hi[:]),
                                      ALU.subtract).then_inc(w_lo_ready, 1)
                    if n == 0:
                        ln.dve_normalise(dve, 0)
                        dve.wait_ge(small_loaded, 16 * len(small))
                        if w["fill"] == "additive":
                            dve.tensor_scalar(mask1[:], adj2[:], -1.0, 1.0, ALU.mult, ALU.add)\
                                .then_inc(mask_steps, 1)
                            dve.wait_ge(mask_steps, 1)
                            dve.tensor_scalar(mask[:], mask1[:], -1e9, None, ALU.mult)\
                                .then_inc(mask_steps, 1)
                        else:
                            dve.tensor_scalar(mask[:], adj2[:], 0.0, MASKED, ALU.is_equal, ALU.mult)\
                                .then_inc(mask_steps, 2)
                        dve.wait_ge(mask_steps, 2)

                def sr(par, r):
                    return s[:, par, r, :, :, :].rearrange("p t m k -> p (t m) k")

                def sums(i, par, r):
                    dve.wait_ge(p_exp, i * R + r + 1)
                    dve.reduce_sum(total[:, r, :], sr(par, r), AX.X).then_inc(p_total, 1)
                    dve.wait_ge(p_total, i * R + r + 1)
                    dve.reciprocal(rtotal[:, r, :], total[:, r, :]).then_inc(p_rtotal, 1)

                def body(i, par):
                    if isinstance(i, int) and i == -1:
                        for f in range(FT):
                            ln.dve_low(dve, 0, f, ring[:, f, :])
                        chunk_loaded(1)
                        ln.dve_stats(dve, 1)
                        ln.dve_normalise(dve, 1)
                        return
                    if isinstance(i, int) and i == 0 and first_load is not None:
                        dve.wait_ge(x_loaded[2], 16)
                    if exists(i + 2):
                        ln.dve_stats(dve, i + 2)
                    if exists(i):
                        for r in range(R):
                            dve.wait_ge(s_ready, i * R + r + 1)
                            dve.scalar_tensor_tensor(
                                sr(par, r), scores[:, r, :].rearrange("p (a k) -> p a k", k=N), SCALE,
                                mask[:].unsqueeze(1).to_broadcast([P, CT * 2, N]),
                                ALU.mult, ALU.add).then_inc(s_masked, 1)
                            dve.wait_ge(s_masked, i * R + r + 1)
                            dve.reduce_max(mx[:, r, :], sr(par, r), AX.X).then_inc(s_max, 1)
                        sums(i, par, 0)
                    if exists(i + 1):
                        for f in range(FT):
                            ln.dve_low(dve, i + 1, f, ring[:, f, :])
                    if exists(i):
                        sums(i, par, 1)
                        sums(i, par, 2)
                    if exists(i - 1):
                        c = i - 1
                        for m in range(FT):
                            dve.wait_ge(oT_hi_ready, c * FT + m + 1)
                            if "bq" in w:
                                ins = dve.scalar_tensor_tensor(oT.lo[:, m, :], ring[:, 2 + m, :],
                                                               col_bias[:, 2, m:m + 1], f32(oT.hi[:, m, :]),
                                                               ALU.add, ALU.subtract)
                            else:
                                ins = dve.tensor_tensor(oT.lo[:, m, :], ring[:, 2 + m, :],
                                                        f32(oT.hi[:, m, :]), ALU.subtract)
                            ins.then_inc(oT_lo_ready, 1)
                    if exists(i):
                        sums(i, par, 3)
                    if tail_norm and exists(i - 2):
                        c = i - 2
                        dve.wait_ge(o_rstd_ready, c + 1)
                        wait(dve, x_final, c)
                        for t in range(CT):
                            last = dve.tensor_scalar(o_n[:, t, :], o[:, t, :], o_mv[:, t, 0:1],
                                                     o_rstd[:, t:t + 1], ALU.subtract, ALU.mult)
                        last.then_inc(o_n_ready, 1)
                    if exists(i + 2):
                        ln.dve_normalise(dve, i + 2)
                    if exists(i - 1):
                        c = i - 1
                        if not tail_norm:
                            dve.wait_ge(x_biased, c + 1)
                        else:
                            wait(dve, x_plus_o, c)
                            wait(dve, o_n_ready, c)
                        for g in range(2):
                            dve.wait_ge(out_ready, c * 2 + g + 1)
                            ob = ring[:, g, :].rearrange("p (t c) -> p t c", t=2)
                            if tail_norm:
                                dve.tensor_tensor(o[:, 2 * g:2 * g + 2, :], ob,
                                                  out_bias[:].unsqueeze(1).to_broadcast([P, 2, D]),
                                                  ALU.add).then_inc(x_done, 1)
                            else:
                                xc = x[:, bass.ds(c * CT + 2 * g, 2), :]
                                dve.tensor_tensor(xc, xc, ob, ALU.add).then_inc(x_done, 1)
                        if tail_norm:
                            dve.wait_ge(x_done, c * 2 + 2)
                            for t in range(CT):
                                last = dve.bn_stats(o_stats[:, t, :], o[:, t, :])
                            last.then_inc(o_bn, 1)
                            ln.dve_carry(dve, o_bn, c + 1)
                            for t in range(CT):
                                last = dve.bn_aggr(o_mv[:, t, :], o_stats[:, t, :])
                            last.then_inc(o_mv_ready, 1)
                    if tail_norm and exists(i - 2):
                        c = i - 2
                        dve.wait_ge(o_ln_ready, c + 1)
                        dve.wait_ge(x_plus_o, c + 1)
                        xc = x[:, bass.ds(c * CT, CT), :]
                        dve.tensor_tensor(xc, xc, o_n[:], ALU.add).then_inc(x_final, 1)

                iterations(dve, body)

            @block.tensor
            def _(pe):
                def columns(parts_, m):
                    return [pair(parts_, slice(None), k, slice(m * P, (m + 1) * P)) for k in range(FT)]

                hT_moving = [pair(hT, slice(None), k, slice(None)) for k in range(FT)]

                def body(i, par):
                    if exists(i):
                        pe.wait_ge(qk_copied, (i + 1) * 2 * FT)
                        wait(pe, s_masked, i * R)
                        for r in range(R):
                            rows = slice(r * HD, (r + 1) * HD)
                            for t in range(CT):
                                for m in range(2):
                                    for g in range(2):
                                        tok = slice(t * P + g * N, t * P + (g + 1) * N)
                                        last = pe.matmul(
                                            scores[g * N:(g + 1) * N, r, (2 * t + m) * N:(2 * t + m + 1) * N],
                                            qT[rows, m, tok], kT[rows, m, tok], start=True, stop=True)
                            last.then_inc(s_ready, 1)
                    if exists(i - 1):
                        c = i - 1
                        wait(pe, x_done, c * 2)
                        pe.wait_ge(v_copied, 2 * CHUNKS if isinstance(i, int) and i >= CHUNKS else (i + 1) * 2)
                        for r in range(R):
                            pe.wait_ge(p_ready, c * R + r + 1)
                            for t in range(CT):
                                last = pe.transpose(
                                    ring[:, r, t * P:(t + 1) * P],
                                    s[:, 1 - par, r, t, :, :].rearrange("p m k -> p (m k)"), ident[:])
                            last.then_inc(pT_ready, 1)
                    if exists(i + 1):
                        for f in range(FT):
                            if exists(i - 1):
                                pe.wait_ge(pT_copied, (i - 1) * R + f + 1)
                            ln.pe_transpose(pe, i + 1, f, ring[:, f, :])
                    if exists(i - 1):
                        c = i - 1
                        wait_apart(pe, pT_copied, i * R)
                        for m in range(FT):
                            rows = slice(m * N, (m + 1) * N)
                            for t in range(CT):
                                for g in range(2):
                                    for r in range(R):
                                        tok = slice(t * P + g * N, t * P + (g + 1) * N)
                                        last = pe.matmul(
                                            ring[r * HD:(r + 1) * HD, 2 + m, tok],
                                            v[rows, 1 - par, t, g, r * HD:(r + 1) * HD],
                                            pT[rows, r, t, g * N:(g + 1) * N], start=True, stop=True)
                            last.then_inc(oT_ready, 1)
                    if exists(i + 1):
                        c = i + 1
                        for n, name in enumerate(("q", "k")):
                            if isinstance(i, int) and i == -1:
                                pe.wait_ge(w_lo_ready, n + 1)
                            if n == 0:
                                pe.wait_ge(ln.hT_lo_ready, FT * (c + 1))
                            else:
                                if exists(i - 1):
                                    pe.wait_ge(oT_lo_ready, i * FT)
                                elif i == 0:
                                    pe.wait_ge(v_copied, 2)
                            for m in range(FT):
                                product(pe, ring[:, 2 * n + m, :], columns(parts[name], m), hT_moving)\
                                    .then_inc(qk_ready, 1)
                    if exists(i - 1):
                        c = i - 1
                        if exists(i + 1):
                            pe.wait_ge(qk_copied, (i + 1) * 2 * FT + FT)
                        pe.wait_ge(oT_lo_ready, i * FT)
                        if isinstance(i, int) and i == 1:
                            pe.wait_ge(w_lo_ready, 4)
                        for g in range(2):
                            for t in (2 * g, 2 * g + 1):
                                stat = [pair(oT, slice(None), k, slice(t * P, (t + 1) * P)) for k in range(FT)]
                                mov = [pair(parts["o"], slice(None), k, slice(None)) for k in range(FT)]
                                last = product(pe, ring[:, g, (t % 2) * D:(t % 2 + 1) * D], stat, mov)
                            last.then_inc(out_ready, 1)
                    if exists(i + 1):
                        c = i + 1
                        if isinstance(i, int) and i == -1:
                            pe.wait_ge(w_lo_ready, 4)
                        pe.wait_ge(qk_copied, (c + 1) * 2 * FT)
                        for g in range(2):
                            for t in (2 * g, 2 * g + 1):
                                stat = [pair(hT, slice(None), k, slice(t * P, (t + 1) * P)) for k in range(FT)]
                                mov = [pair(parts["v"], slice(None), k, slice(None)) for k in range(FT)]
                                last = product(pe, ring[:, 2 + g, (t % 2) * D:(t % 2 + 1) * D], stat, mov)
                            last.then_inc(v_ready, 1)

                iterations(pe, body)


def graph_attention_phase(nc, x, ident, psum, a):
    wide, ring = psum
    WX = D + 2
    with Phase(nc) as ctx:
        def sb(name, shape, dt=F32):
            return ctx.enter_context(nc.sbuf_tensor(f"l2_{name}", shape, dt))

        def sem(name):
            return ctx.semaphore(nc, f"l2_{name}")

        ln = LayerNorm(nc, ctx, "l2", x, ident)
        hT = ln.hT
        w_ext = sb("w_ext", [P, FT, WX])
        w = Parts(ctx, nc, "l2_w", [P, FT, WX])
        wa2 = Parts(ctx, nc, "l2_wa2", [P, FT, P])
        a_rows = sb("a_rows", [P, 2, D])
        wa_terms = sb("wa_terms", [P, 2, FT, D])
        adj2 = sb("adj2", [P, N])
        beta = sb("beta", [P, 1])
        hw = sb("hw", [P, 2, CT, WX])
        e = sb("e", [P, CT, N])
        e_lrelu = sb("e_lrelu", [P, CT, N])
        mx = sb("mx", [P, CT])
        total = sb("total", [P, CT])
        rtotal = sb("rtotal", [P, CT])
        att = sb("att", [P, CT, 2, N])
        attT = sb("attT", [P, CT, P])
        y = sb("y", [P, CT, D])
        y_neg = sb("y_neg", [P, CT, D])
        y_pos = sb("y_pos", [P, CT, D])

        w_loaded = sem("w_loaded")
        small_loaded = sem("small_loaded")
        wa_steps = sem("wa_steps")
        w_hi_ready = sem("w_hi_ready")
        w_lo_ready = sem("w_lo_ready")
        att_cleared = sem("att_cleared")
        s2_ready = sem("s2_ready")
        hw_ready = sem("hw_ready")
        hw_copied = sem("hw_copied")
        e_sum = sem("e_sum")
        e_leaky = sem("e_leaky")
        e_masked = sem("e_masked")
        e_max = sem("e_max")
        e_shifted = sem("e_shifted")
        e_exp = sem("e_exp")
        e_total = sem("e_total")
        e_rtotal = sem("e_rtotal")
        att_ready = sem("att_ready")
        attT_ready = sem("attT_ready")
        attT_copied = sem("attT_copied")
        agg_ready = sem("agg_ready")
        y_ready = sem("y_ready")
        y_neg_ready = sem("y_neg_ready")
        y_exp_ready = sem("y_exp_ready")
        y_pos_ready = sem("y_pos_ready")
        x_plus_pos = sem("x_plus_pos")
        x_done = sem("x_done")

        def iterations(eng, body):
            for i in (-1, 0):
                body(i, i % 2)
            with eng.Fori(0, (CHUNKS - 4) // 2) as j:
                body(j * 2 + 1, 1)
                body(j * 2 + 2, 0)
            for i in range(CHUNKS - 3, CHUNKS):
                body(i, i % 2)

        with nc.Block() as block:
            @block.sync
            def _(sp):
                sp.dma_start(w_ext[:, :, 0:D], a["L2_gnn_W"].rearrange("(k p) n -> p k n", p=P)).then_inc(w_loaded, 16)
                for n in range(2):
                    row = a["L2_gnn_a"][n * D:(n + 1) * D, :].rearrange("n a -> (n a)")
                    sp.dma_start(a_rows[:, n, :], spread_rows(row, P)).then_inc(small_loaded, 16)
                for g in range(2):
                    sp.dma_start(adj2[g * N:(g + 1) * N, :], a["adj"]).then_inc(small_loaded, 16)
                sp.dma_start(beta[:], spread_rows(a["L2_gnn_beta"], P)).then_inc(small_loaded, 16)

            @block.gpsimd
            def _(pool):
                ln.pool_setup(pool)
                pool.memset(att[:], 0.0).then_inc(att_cleared, 1)
                pool.wait_ge(att_cleared, 1)

                def body(i, par):
                    if isinstance(i, int) and i == -1:
                        ln.pool_rstd(pool, 0)
                        ln.pool_rstd(pool, 1)
                    elif exists(i + 2):
                        ln.pool_rstd(pool, i + 2)
                    if exists(i + 1):
                        c = i + 1
                        pool.wait_ge(e_max, c + 1)
                        pool.tensor_tensor(e[:], e[:], mx[:].unsqueeze(2).to_broadcast([P, CT, N]),
                                           ALU.subtract).then_inc(e_shifted, 1)
                    if exists(i):
                        pool.wait_ge(y_pos_ready, i + 1)
                        xc = x[:, bass.ds(i * CT, CT), :]
                        pool.tensor_tensor(xc, xc, y_pos[:], ALU.add).then_inc(x_plus_pos, 1)

                iterations(pool, body)

            @block.scalar
            def _(act):
                act.wait_ge(wa_steps, 2)
                act.activation(w.hi[:], w_ext[:], ACT.Copy).then_inc(w_hi_ready, 1)
                act.activation(wa2.hi[:], w_ext[:, :, D + 1:D + 2].to_broadcast([P, FT, P]), ACT.Copy)\
                    .then_inc(w_hi_ready, 1)

                def body(i, par):
                    if exists(i + 1):
                        for f in range(FT):
                            ln.act_high(act, i + 1, f, ring[:, f, :])
                    if exists(i):
                        act.wait_ge(attT_ready, i + 1)
                        act.activation(attT[:].rearrange("p t q -> p (t q)"), ring[:, 3, :], ACT.Copy)\
                            .then_inc(attT_copied, 1)
                    if exists(i + 1):
                        for t in range(CT):
                            act.wait_ge(hw_ready, (i + 1) * CT + t + 1)
                            act.activation(hw[:, 1 - par, t, :], wide[:, t, 0:WX], ACT.Copy)\
                                .then_inc(hw_copied, 1)
                        act.wait_ge(e_shifted, i + 2)
                        act.activation(e[:], e[:], ACT.Exp).then_inc(e_exp, 1)
                    if exists(i):
                        act.wait_ge(y_neg_ready, i + 1)
                        act.activation(y_neg[:], y_neg[:], ACT.Exp).then_inc(y_exp_ready, 1)

                iterations(act, body)

            @block.vector
            def _(dve):
                ln.dve_stats(dve, 0)
                dve.wait_ge(att_cleared, 1)
                ln.dve_normalise(dve, 0)
                dve.wait_ge(w_loaded, 16)
                dve.wait_ge(small_loaded, 16 * 5)
                for n in range(2):
                    last = dve.tensor_tensor(wa_terms[:, n, :, :], w_ext[:, :, 0:D],
                                             a_rows[:, n, :].unsqueeze(1).to_broadcast([P, FT, D]), ALU.mult)
                last.then_inc(wa_steps, 1)
                dve.wait_ge(wa_steps, 1)
                for n in range(2):
                    last = dve.reduce_sum(w_ext[:, :, D + n], wa_terms[:, n, :, :], AX.X)
                last.then_inc(wa_steps, 1)
                dve.wait_ge(w_hi_ready, 1)
                dve.tensor_tensor(w.lo[:], w_ext[:], f32(w.hi[:]), ALU.subtract).then_inc(w_lo_ready, 1)
                dve.wait_ge(w_hi_ready, 2)
                dve.tensor_tensor(wa2.lo[:], w_ext[:, :, D + 1:D + 2].to_broadcast([P, FT, P]), f32(wa2.hi[:]),
                                  ALU.subtract).then_inc(w_lo_ready, 1)

                def body(i, par):
                    if isinstance(i, int) and i == -1:
                        ln.dve_stats(dve, 1)
                    elif exists(i + 2):
                        ln.dve_stats(dve, i + 2)
                    if exists(i + 1):
                        c = i + 1
                        for f in range(FT):
                            ln.dve_low(dve, c, f, ring[:, f, :])
                        if exists(i + 2) and not (isinstance(i, int) and i == -1):
                            ln.dve_normalise(dve, i + 2)
                        if isinstance(i, int) and i == -1:
                            ln.dve_normalise(dve, 1)
                        dve.wait_ge(s2_ready, c + 1)
                        dve.wait_ge(hw_copied, (c + 1) * CT)
                        wait(dve, att_ready, c)
                        for g in range(2):
                            rows = slice(g * N, (g + 1) * N)
                            s2 = ring[rows, 2, :].rearrange("p (t g j) -> p t g j", g=2, j=N)[:, :, g, :]
                            last = dve.tensor_tensor(e[rows, :, :], s2,
                                                     hw[rows, 1 - par, :, D:D + 1].to_broadcast([N, CT, N]), ALU.add)
                        last.then_inc(e_sum, 1)
                        dve.wait_ge(e_sum, c + 1)
                        dve.scalar_tensor_tensor(e_lrelu[:], e[:], ALPHA, e[:], ALU.mult, ALU.max).then_inc(e_leaky, 1)
                        dve.wait_ge(e_leaky, c + 1)
                        dve.tensor_tensor(e[:], e_lrelu[:], adj2[:].unsqueeze(1).to_broadcast([P, CT, N]), ALU.mult)\
                            .then_inc(e_masked, 1)
                        dve.wait_ge(e_masked, c + 1)
                        dve.reduce_max(mx[:], e[:], AX.X).then_inc(e_max, 1)
                    if exists(i):
                        wait(dve, x_done, i)
                        for g in range(2):
                            dve.wait_ge(agg_ready, i * 2 + g + 1)
                            dve.scalar_tensor_tensor(y[:, 2 * g:2 * g + 2, :], hw[:, par, 2 * g:2 * g + 2, 0:D],
                                                     beta[:, 0:1],
                                                     ring[:, g, :].rearrange("p (t c) -> p t c", t=2),
                                                     ALU.mult, ALU.add).then_inc(y_ready, 1)
                        dve.wait_ge(y_ready, (i + 1) * 2)
                        dve.tensor_scalar(y_neg[:], y[:], 0.0, None, ALU.min).then_inc(y_neg_ready, 1)
                        dve.tensor_scalar(y_pos[:], y[:], 0.0, -1.0, ALU.max, ALU.add).then_inc(y_pos_ready, 1)
                    if exists(i + 1):
                        c = i + 1
                        dve.wait_ge(e_exp, c + 1)
                        dve.reduce_sum(total[:], e[:], AX.X).then_inc(e_total, 1)
                        dve.wait_ge(e_total, c + 1)
                        dve.reciprocal(rtotal[:], total[:]).then_inc(e_rtotal, 1)
                        dve.wait_ge(e_rtotal, c + 1)
                        wait(dve, attT_ready, c)
                        for g in range(2):
                            rows = slice(g * N, (g + 1) * N)
                            last = dve.tensor_tensor(att[rows, :, g, :], e[rows, :, :],
                                                     rtotal[rows, :].unsqueeze(2).to_broadcast([N, CT, N]), ALU.mult)
                        last.then_inc(att_ready, 1)
                    if exists(i):
                        dve.wait_ge(y_exp_ready, i + 1)
                        dve.wait_ge(x_plus_pos, i + 1)
                        xc = x[:, bass.ds(i * CT, CT), :]
                        dve.tensor_tensor(xc, xc, y_neg[:], ALU.add).then_inc(x_done, 1)

                iterations(dve, body)

            @block.tensor
            def _(pe):
                hT_moving = [pair(hT, slice(None), k, slice(None)) for k in range(FT)]

                def body(i, par):
                    if exists(i + 1):
                        if exists(i):
                            wait(pe, y_ready, i * 2)
                        for f in range(FT):
                            ln.pe_transpose(pe, i + 1, f, ring[:, f, :])
                    if exists(i):
                        pe.wait_ge(att_ready, i + 1)
                        for t in range(CT):
                            last = pe.transpose(ring[:, 3, t * P:(t + 1) * P],
                                                att[:, t, :, :].rearrange("p g j -> p (g j)"), ident[:])
                        last.then_inc(attT_ready, 1)
                    if exists(i + 1):
                        c = i + 1
                        if isinstance(i, int) and i == -1:
                            pe.wait_ge(w_lo_ready, 2)
                        pe.wait_ge(ln.hT_lo_ready, (c + 1) * FT)
                        wait(pe, hw_copied, c * CT)
                        for t in range(CT):
                            stat = [pair(hT, slice(None), k, slice(t * P, (t + 1) * P)) for k in range(FT)]
                            mov = [pair(w, slice(None), k, slice(None)) for k in range(FT)]
                            product(pe, wide[:, t, 0:WX], stat, mov).then_inc(hw_ready, 1)
                        product(pe, ring[:, 2, :], [pair(wa2, slice(None), k, slice(None)) for k in range(FT)],
                                hT_moving).then_inc(s2_ready, 1)
                    if exists(i):
                        pe.wait_ge(attT_copied, i + 1)
                        if exists(i + 1):
                            pe.wait_ge(ln.hT_lo_ready, (i + 2) * FT)
                        else:
                            pe.wait_ge(y_ready, i * 2)
                        for g in range(2):
                            for t in (2 * g, 2 * g + 1):
                                last = pe.matmul(ring[:, g, (t % 2) * D:(t % 2 + 1) * D], attT[:, t, :],
                                                 hw[:, par, t, 0:D], start=True, stop=True)
                            last.then_inc(agg_ready, 1)

                iterations(pe, body)


def recurrence_phase(nc, x, ident, psum, a, out):
    bank_a, bank_b = psum
    ring, high = bank_b, bank_a
    GROUPS = CHUNKS // 2
    HALVES = 2 * STEPS
    with Phase(nc) as ctx:
        def sb(name, shape, dt=F32):
            return ctx.enter_context(nc.sbuf_tensor(f"l3_{name}", shape, dt))

        def sem(name):
            return ctx.semaphore(nc, f"l3_{name}")

        ln = LayerNorm(nc, ctx, "l3", x, ident, transposed=False)
        mats = ["w3", "w4", "w5", "u3", "u5"]
        wT = {m: Parts(ctx, nc, f"l3_{m}", [P, FT, D]) for m in mats}
        w_stage = sb("w_stage", [P, 3, FT, 2 * D])
        u_stage = sb("u_stage", [P, 2, FT, D])
        b_stage = sb("b_stage", [P, 5, FT])
        bias = sb("bias", [P, 3, FT])
        adjT = sb("adjT", [P, P])
        adj = Parts(ctx, nc, "l3_adj", [P, P])
        h0 = [sb(f"h0_{q}", [P, FT, CW]) for q in "ab"]
        h = [sb(f"h_{q}", [P, FT, CW]) for q in "ab"]
        hp = [Parts(ctx, nc, f"l3_hp_{q}", [P, FT, CW]) for q in "ab"]
        tok = Parts(ctx, nc, "l3_tok", [P, CT, D])
        agg = Parts(ctx, nc, "l3_agg", [P, FT, CW])
        hu = sb("hu", [P, FT, CW])
        r = sb("r", [P, FT, CW])
        z = sb("z", [P, FT, CW])
        hv = sb("hv", [P, FT, CW])
        rh = sb("rh", [P, FT, CW])
        rhp = Parts(ctx, nc, "l3_rhp", [P, FT, CW])

        adj_cleared = sem("adj_cleared")
        adj_loaded = sem("adj_loaded")
        w_loaded = sem("w_loaded")
        b_loaded = sem("b_loaded")
        halves_added = sem("halves_added")
        b_ready = sem("b_ready")
        wT_ready = sem("wT_ready")
        wT_hi_ready = sem("wT_hi_ready")
        wT_lo_ready = sem("wT_lo_ready")
        tok_ready = sem("tok_ready")
        tok_hi_ready = sem("tok_hi_ready")
        tok_lo_ready = sem("tok_lo_ready")
        hu_ready = sem("hu_ready")
        hu_copied = sem("hu_copied")
        agg_ready = sem("agg_ready")
        agg_hi_ready = sem("agg_hi_ready")
        agg_lo_ready = sem("agg_lo_ready")
        r_ready = sem("r_ready")
        r_added = sem("r_added")
        r_done = sem("r_done")
        z_ready = sem("z_ready")
        z_added = sem("z_added")
        z_done = sem("z_done")
        rh_done = sem("rh_done")
        rh_hi_ready = sem("rh_hi_ready")
        rh_lo_ready = sem("rh_lo_ready")
        hv_ready = sem("hv_ready")
        hv_done = sem("hv_done")
        hv_minus_h = sem("hv_minus_h")
        hv_gated = sem("hv_gated")
        h_done = sem("h_done")
        h_hi_ready = sem("h_hi_ready")
        h_lo_ready = sem("h_lo_ready")
        h0_hi_ready = sem("h0_hi_ready")
        h0_lo_ready = sem("h0_lo_ready")
        final_ready = sem("final_ready")
        x_done = sem("x_done")
        stored = sem("stored")

        class Half:

            def __init__(self, g, k):
                fixed = isinstance(g, int)
                self.n = g * HALVES + k
                self.k = k % HALVES
                self.first = fixed and self.n == 0
                self.last = fixed and self.n == GROUPS * HALVES
                self.step = self.k // 2
                self.stops = fixed and g == GROUPS - 1
                self.me = self.k % 2
                self.other = 1 - self.me
                group = g + 1 if k == HALVES else g
                self.chunk = group * 2 + self.me
                self.enters = self.leaves = self.left = None
                if self.k == HALVES - 1:
                    if not (fixed and group == GROUPS - 1):
                        self.enters = group * 2 + 2
                    self.leaves = group * 2
                if self.k == 0:
                    if not self.last:
                        self.enters = group * 2 + 1
                    if not self.first:
                        self.leaves = group * 2 - 1
                if self.k == 0 and not self.first:
                    self.left = group * 2 - 2
                self.later = group * (HALVES - 2) + self.k
                self.before_step = STEPS - 1 if self.k == 0 else (self.k - 1) // 2
                self.before_later = self.later

            def h_me(self):
                return h0[self.me] if self.step == 0 else h[self.me]

            def h_before(self):
                return h0[self.other] if self.before_step == 0 else h[self.other]

        def halves(eng, body):
            body(Half(0, 0))
            with eng.Fori(0, GROUPS - 1) as g:
                for k in range(1, HALVES + 1):
                    body(Half(g, k))
            for k in range(1, HALVES + 1):
                body(Half(GROUPS - 1, k))

        with nc.Block() as block:
            @block.sync
            def _(sp):
                for n, m in enumerate(("w3", "w4", "w5")):
                    sp.dma_start(w_stage[:, n, :, :], a[f"L3_gnn_{m}_w"].rearrange("(o p) i -> p o i", p=P))\
                        .then_inc(w_loaded, 16)
                for n, m in enumerate(("u3", "u5")):
                    sp.dma_start(u_stage[:, n, :, :], a[f"L3_gnn_{m}_w"].rearrange("(o p) i -> p o i", p=P))\
                        .then_inc(w_loaded, 16)
                for n, m in enumerate(mats):
                    sp.dma_start(b_stage[:, n, :], load_columns(a[f"L3_gnn_{m}_b"])).then_inc(b_loaded, 16)
                sp.wait_ge(adj_cleared, 1)
                for g in range(2):
                    sp.dma_start(adjT[g * N:(g + 1) * N, g * N:(g + 1) * N], a["adj"].rearrange("i j -> j i"))\
                        .then_inc(adj_loaded, 16)
                dst = out.rearrange("b n d -> (b n) d").rearrange("(t p) d -> p t d", p=P)
                with sp.Fori(0, CHUNKS) as c:
                    sp.wait_ge(x_done, c * 2 + 2)
                    sp.dma_start(dst[:, bass.ds(c * CT, CT), :], x[:, bass.ds(c * CT, CT), :]).then_inc(stored, 16)
                sp.wait_ge(stored, 16 * CHUNKS)

            @block.gpsimd
            def _(pool):
                ln.pool_setup(pool)
                pool.memset(adjT[:], 0.0).then_inc(adj_cleared, 1)
                ln.pool_rstd(pool, 0)
                with pool.Fori(1, CHUNKS) as c:
                    ln.pool_rstd(pool, c)

            @block.scalar
            def _(act):
                for n, m in enumerate(mats):
                    act.wait_ge(wT_ready, n + 1)
                    bank = ring[:, n, :] if n < 4 else high[:, 0, :]
                    act.activation(wT[m].hi[:], bank.rearrange("p (k o) -> p k o", k=FT), ACT.Copy)\
                        .then_inc(wT_hi_ready, 1)
                act.wait_ge(adj_loaded, 32)
                act.activation(adj.hi[:], adjT[:], ACT.Copy).then_inc(wT_hi_ready, 1)
                act.wait_ge(b_ready, 3)

                def enter(c, me):
                    for f in range(FT):
                        act.wait_ge(ln.xT_ready, c * FT + f + 1)
                        act.activation(hp[me].hi[:, f, :], ring[:, 2 + f, :], ACT.Relu)
                        act.activation(h0[me][:, f, :], ring[:, 2 + f, :], ACT.Relu).then_inc(h0_hi_ready, 1)

                def body(s):
                    n = s.n
                    if not s.last:
                        for q in range(2):
                            act.wait_ge(tok_ready, n * 2 + q + 1)
                            act.activation(tok.hi[:, 2 * q:2 * q + 2, :],
                                           ring[:, q, :].rearrange("p (t d) -> p t d", t=2), ACT.Copy)\
                                .then_inc(tok_hi_ready, 1)
                    if not s.first:
                        for m in range(FT):
                            act.wait_ge(z_added, (n - 1) * FT + m + 1)
                            act.activation(z[:, m, :], z[:, m, :], ACT.Sigmoid, bias=bias[:, 0, m:m + 1])\
                                .then_inc(z_done, 1)
                    if not s.last:
                        act.wait_ge(hu_ready, n * FT + 1)
                        act.activation(hu[:, 0, :], ring[:, 2, :], ACT.Copy).then_inc(hu_copied, 1)
                    if not s.first:
                        act.wait_ge(rh_done, n)
                        act.activation(rhp.hi[:], rh[:], ACT.Copy).then_inc(rh_hi_ready, 1)
                    if not s.last:
                        act.wait_ge(hu_ready, (n + 1) * FT)
                        act.activation(hu[:, 1, :], ring[:, 3, :], ACT.Copy).then_inc(hu_copied, 1)
                        for m in range(FT):
                            act.wait_ge(agg_ready, n * FT + m + 1)
                            act.activation(agg.hi[:, m, :], high[:, m, :], ACT.Copy).then_inc(agg_hi_ready, 1)
                    if not s.first:
                        for m in range(FT):
                            act.wait_ge(hv_ready, (n - 1) * FT + m + 1)
                            act.activation(hv[:, m, :], high[:, 2 + m, :], ACT.Tanh, bias=bias[:, 2, m:m + 1])\
                                .then_inc(hv_done, 1)
                    if s.enters is not None:
                        enter(s.enters, s.other)
                    for m in range(FT):
                        if not s.first:
                            act.wait_ge(h_done, (n - 1) * FT + m + 1)
                            if s.before_step < STEPS - 1:
                                act.activation(hp[s.other].hi[:, m, :], h[s.other][:, m, :], ACT.Copy)\
                                    .then_inc(h_hi_ready, 1)
                    for m in range(FT):
                        if not s.last:
                            act.wait_ge(r_added, n * FT + m + 1)
                            act.activation(r[:, m, :], r[:, m, :], ACT.Sigmoid, bias=bias[:, 1, m:m + 1])\
                                .then_inc(r_done, 1)

                enter(0, 0)
                halves(act, body)

            @block.vector
            def _(dve):
                ln.dve_stats(dve, 0)
                dve.wait_ge(w_loaded, 16 * 5)
                dve.tensor_tensor(w_stage[:, :, :, 0:D], w_stage[:, :, :, 0:D], w_stage[:, :, :, D:2 * D], ALU.add)\
                    .then_inc(halves_added, 1)
                ln.dve_normalise(dve, 0)
                dve.wait_ge(b_loaded, 16 * 5)
                for n, (wb, ub) in enumerate(((0, 3), (1, 3), (2, 4))):
                    dve.tensor_tensor(bias[:, n, :], b_stage[:, wb, :], b_stage[:, ub, :], ALU.add).then_inc(b_ready, 1)
                for n, m in enumerate(mats):
                    dve.wait_ge(wT_hi_ready, n + 1)
                    bank = ring[:, n, :] if n < 4 else high[:, 0, :]
                    dve.tensor_tensor(wT[m].lo[:], bank.rearrange("p (k o) -> p k o", k=FT), f32(wT[m].hi[:]),
                                      ALU.subtract).then_inc(wT_lo_ready, 1)
                dve.wait_ge(wT_hi_ready, 6)
                dve.tensor_tensor(adj.lo[:], adjT[:], f32(adj.hi[:]), ALU.subtract).then_inc(wT_lo_ready, 1)

                def enter(c, me):
                    for f in range(FT):
                        dve.wait_ge(h0_hi_ready, c * FT + f + 1)
                        dve.scalar_tensor_tensor(hp[me].lo[:, f, :], ring[:, 2 + f, :], 0.0,
                                                 f32(hp[me].hi[:, f, :]), ALU.max, ALU.subtract)\
                            .then_inc(h0_lo_ready, 1)

                def leave(c):
                    for q in range(2):
                        dve.wait_ge(final_ready, c * 2 + q + 1)
                        xc = x[:, bass.ds(c * CT + 2 * q, 2), :]
                        dve.tensor_tensor(xc, xc, ring[:, 2 + q, :].rearrange("p (t d) -> p t d", t=2),
                                          ALU.add).then_inc(x_done, 1)

                def body(s):
                    n = s.n
                    if s.left is not None:
                        leave(s.left)
                    if not s.last:
                        for q in range(2):
                            dve.wait_ge(tok_hi_ready, n * 2 + q + 1)
                            dve.tensor_tensor(tok.lo[:, 2 * q:2 * q + 2, :],
                                              ring[:, q, :].rearrange("p (t d) -> p t d", t=2),
                                              f32(tok.hi[:, 2 * q:2 * q + 2, :]), ALU.subtract)\
                                .then_inc(tok_lo_ready, 1)
                    old, new = s.h_before(), h[s.other]
                    if not s.first:
                        dve.wait_ge(r_done, n * FT)
                        dve.tensor_tensor(rh[:], r[:], old[:], ALU.mult).then_inc(rh_done, 1)
                        dve.wait_ge(rh_hi_ready, n)
                        dve.tensor_tensor(rhp.lo[:], rh[:], f32(rhp.hi[:]), ALU.subtract).then_inc(rh_lo_ready, 1)
                    if not s.last:
                        for m in range(FT):
                            dve.wait_ge(agg_hi_ready, n * FT + m + 1)
                            dve.tensor_tensor(agg.lo[:, m, :], high[:, m, :], f32(agg.hi[:, m, :]),
                                              ALU.subtract).then_inc(agg_lo_ready, 1)
                    if s.k == 1 and not s.stops:
                        ln.dve_stats(dve, s.chunk + 1)
                    if s.k == 2 and not s.stops:
                        ln.dve_normalise(dve, s.chunk + 2)
                    if s.k == 3 and not s.stops:
                        ln.dve_stats(dve, s.chunk + 2)
                    if not s.first:
                        dve.wait_ge(z_done, n * FT)
                        for m in range(FT):
                            dve.wait_ge(hv_done, (n - 1) * FT + m + 1)
                            dve.tensor_tensor(hv[:, m, :], hv[:, m, :], old[:, m, :], ALU.subtract)\
                                .then_inc(hv_minus_h, 1)
                            dve.wait_ge(hv_minus_h, (n - 1) * FT + m + 1)
                            dve.tensor_tensor(hv[:, m, :], hv[:, m, :], z[:, m, :], ALU.mult).then_inc(hv_gated, 1)
                            dve.wait_ge(hv_gated, (n - 1) * FT + m + 1)
                            dve.tensor_tensor(new[:, m, :], old[:, m, :], hv[:, m, :], ALU.add).then_inc(h_done, 1)
                    if not s.last:
                        dve.wait_ge(hu_copied, (n + 1) * FT)
                        for m in range(FT):
                            dve.wait_ge(r_ready, n * FT + m + 1)
                            dve.tensor_tensor(r[:, m, :], ring[:, m, :], hu[:, m, :], ALU.add).then_inc(r_added, 1)
                    if s.enters is not None:
                        enter(s.enters, s.other)
                    if not s.first and s.before_step < STEPS - 1:
                        for m in range(FT):
                            dve.wait_ge(h_hi_ready, (s.before_later - 1) * FT + m + 1)
                            dve.tensor_tensor(hp[s.other].lo[:, m, :], h[s.other][:, m, :],
                                              f32(hp[s.other].hi[:, m, :]), ALU.subtract).then_inc(h_lo_ready, 1)
                    if s.k == 5 and s.enters is not None:
                        ln.dve_normalise(dve, s.chunk + 2)
                    if not s.last:
                        for m in range(FT):
                            dve.wait_ge(z_ready, n * FT + m + 1)
                            dve.tensor_tensor(z[:, m, :], high[:, m, :], hu[:, m, :], ALU.add).then_inc(z_added, 1)
                    if s.k == 0 and s.leaves is not None:
                        leave(s.leaves)

                enter(0, 0)
                ln.dve_stats(dve, 1)
                ln.dve_normalise(dve, 1)
                halves(dve, body)

            @block.tensor
            def _(pe):
                def columns(parts_, m):
                    return [pair(parts_, slice(None), k, slice(m * P, (m + 1) * P)) for k in range(FT)]

                def moving(parts_):
                    return [pair(parts_, slice(None), k, slice(None)) for k in range(FT)]

                def enter(c):
                    for f in range(FT):
                        ln.pe_transpose(pe, c, f, ring[:, 2 + f, :])

                pe.wait_ge(halves_added, 1)
                for n, m in enumerate(mats):
                    bank = ring[:, n, :] if n < 4 else high[:, 0, :]
                    for k in range(FT):
                        for o in range(FT):
                            src = w_stage[:, n, o, k * P:(k + 1) * P] if n < 3 else u_stage[:, n - 3, o, k * P:(k + 1) * P]
                            last = pe.transpose(bank[:, k * D + o * P:k * D + (o + 1) * P], src, ident[:])
                    last.then_inc(wT_ready, 1)
                pe.wait_ge(wT_lo_ready, 6)

                def body(s):
                    n = s.n
                    if not s.last:
                        if s.step == 0:
                            pe.wait_ge(h0_hi_ready, (s.chunk + 1) * FT)
                        else:
                            pe.wait_ge(h_done, (n - 1) * FT)
                        if not s.first:
                            pe.wait_ge(r_added, n * FT)
                        for q in range(2):
                            for t in (2 * q, 2 * q + 1):
                                for f in range(FT):
                                    at = (t % 2) * D + f * P
                                    last = pe.transpose(ring[:, q, at:at + P],
                                                        s.h_me()[:, f, t * P:(t + 1) * P], ident[:])
                            last.then_inc(tok_ready, 1)
                        if s.step == 0:
                            pe.wait_ge(h0_lo_ready, (s.chunk + 1) * FT)
                        else:
                            pe.wait_ge(h_lo_ready, (s.later - 1) * FT)
                        if s.left is not None:
                            pe.wait_ge(x_done, (s.left + 1) * 2)
                        elif s.k == 1:
                            pe.wait_ge(tok_lo_ready, n * 2 + 1)
                        elif not s.first:
                            pe.wait_ge(hu_copied, n * FT)
                        for m in range(FT):
                            product(pe, ring[:, 2 + m, :], columns(wT["u3"], m), moving(hp[s.me])).then_inc(hu_ready, 1)
                        pe.wait_ge(tok_lo_ready, (n + 1) * 2)
                        if not s.first:
                            pe.wait_ge(z_added, n * FT)
                        for m in range(FT):
                            for t in range(CT):
                                last = product(pe, high[:, m, t * P:(t + 1) * P],
                                               [pair(tok, slice(None), t, slice(m * P, (m + 1) * P))],
                                               [(adj.hi[:], adj.lo[:])])
                            last.then_inc(agg_ready, 1)
                    if not s.first:
                        pe.wait_ge(rh_lo_ready, n)
                        for m in range(FT):
                            product(pe, high[:, 2 + m, :], columns(wT["u5"], m), moving(rhp), begins=False)\
                                .then_inc(hv_ready, 1)
                    if s.enters is not None:
                        pe.wait_ge(hu_copied, (n + 1) * FT)
                        enter(s.enters)
                    if not s.last:
                        pe.wait_ge(agg_lo_ready, (n + 1) * FT)
                        for m in range(FT):
                            product(pe, ring[:, m, :], columns(wT["w4"], m), moving(agg)).then_inc(r_ready, 1)
                        for m in range(FT):
                            product(pe, high[:, m, :], columns(wT["w3"], m), moving(agg)).then_inc(z_ready, 1)
                        if not s.first:
                            pe.wait_ge(hv_done, n * FT)
                        for m in range(FT):
                            product(pe, high[:, 2 + m, :], columns(wT["w5"], m), moving(agg), ends=False)
                    if s.leaves is not None:
                        pe.wait_ge(h_done, n * FT)
                        if s.enters is not None:
                            pe.wait_ge(h0_lo_ready, (s.enters + 1) * FT)
                        elif not s.last:
                            pe.wait_ge(hu_copied, (n + 1) * FT)
                        else:
                            pe.wait_ge(x_done, s.leaves * 2)
                        for q in range(2):
                            for t in (2 * q, 2 * q + 1):
                                for f in range(FT):
                                    at = (t % 2) * D + f * P
                                    last = pe.transpose(ring[:, 2 + q, at:at + P],
                                                        h[s.other][:, f, t * P:(t + 1) * P], ident[:])
                            last.then_inc(final_ready, 1)

                enter(0)
                halves(pe, body)


def build(nc, a, out):
    with ExitStack() as ctx:
        x = ctx.enter_context(nc.sbuf_tensor("x", [P, TILES, D], F32))
        ident = ctx.enter_context(nc.sbuf_tensor("ident", [P, P], F32))
        scores = ctx.enter_context(nc.psum_tensor("scores", [P, 4, BANK], F32))
        ring = ctx.enter_context(nc.psum_tensor("ring", [P, 4, BANK], F32))
        ident_steps = ctx.enter_context(nc.semaphore("ident_steps"))
        ctx.enter_context(nc.allow_non_contiguous_dma(reason="small transposed and replicated loads"))
        with nc.Block() as block:
            @block.gpsimd
            def _(pool):
                pool.memset(ident[:], 0.0).then_inc(ident_steps, 1)
                pool.wait_ge(ident_steps, 1)
                pool.affine_select(out=ident[:], in_=ident[:], compare_op=ALU.not_equal, fill=1.0, base=0,
                                   pattern=[[-1, P]], channel_multiplier=1).then_inc(ident_steps, 1)
                pool.wait_ge(ident_steps, 2)

        def rows(ap):
            return ap.rearrange("(k p) n -> p k n", p=P)

        adj = a["adj"]
        attention_phase(nc, "l0", x, ident, (scores, ring), dict(
            adj=adj, wq=rows(a["L0_gnn_Wq"]), wk=rows(a["L0_gnn_Wk"]), wv=rows(a["L0_gnn_Wv"]),
            wo=rows(a["L0_gnn_Wo"]), bq=a["L0_gnn_bq"], bk=a["L0_gnn_bk"], bv=a["L0_gnn_bv"],
            bo=a["L0_gnn_bo"], fill="additive"), first_load=a["x"])
        wqkv = rows(a["L1_gnn_w_qkv"])
        attention_phase(nc, "l1", x, ident, (scores, ring), dict(
            adj=adj, wq=wqkv[:, :, 0:D], wk=wqkv[:, :, D:2 * D], wv=wqkv[:, :, 2 * D:3 * D],
            wo=rows(a["L1_gnn_w_proj"]), bo=a["L1_gnn_b_proj"], fill="exclusive"),
            tail_norm=dict(gamma=a["L1_gnn_ln_gamma"], beta=a["L1_gnn_ln_beta"]))
        graph_attention_phase(nc, x, ident, (scores, ring), a)
        recurrence_phase(nc, x, ident, (scores, ring), a, out)


INPUTS = ["x", "adj", "L0_gnn_Wq", "L0_gnn_bq", "L0_gnn_Wk", "L0_gnn_bk", "L0_gnn_Wv", "L0_gnn_bv",
          "L0_gnn_Wo", "L0_gnn_bo", "L1_gnn_w_qkv", "L1_gnn_w_proj", "L1_gnn_b_proj", "L1_gnn_ln_gamma",
          "L1_gnn_ln_beta", "L2_gnn_W", "L2_gnn_a", "L2_gnn_beta", "L3_gnn_w3_w", "L3_gnn_w3_b",
          "L3_gnn_u3_w", "L3_gnn_u3_b", "L3_gnn_w4_w", "L3_gnn_w4_b", "L3_gnn_w5_w", "L3_gnn_w5_b",
          "L3_gnn_u5_w", "L3_gnn_u5_b"]


def kernel(**inputs):
    import numpy as np
    import concourse.bacc as bacc
    from concourse import mybir as mb
    from concourse.bass_utils import run_bass_kernel_spmd as run

    nc = bacc.Bacc("TRN2", target_bir_lowering=False, num_devices=1)
    arrays, handles = {}, {}
    for name in INPUTS:
        v = np.ascontiguousarray(inputs[name])
        arrays[f"in_{name}"] = v
        handles[name] = nc.dram_tensor(f"in_{name}", v.shape, mb.dt.from_np(v.dtype), kind="ExternalInput").ap()
    out = nc.dram_tensor("out_x", (B, N, D), mb.dt.float32, kind="ExternalOutput").ap()
    build(nc, handles, out)
    result = run(nc, [arrays], core_ids=[0])
    return result.results[0]["out_x"]
```

```python
import concourse.bass as bass
from concourse import mybir
from contextlib import ExitStack
import numpy as np

F32 = mybir.dt.float32
F32R = mybir.dt.float32r
ALU = mybir.AluOpType
ACT = mybir.ActivationFunctionType
AX = mybir.AxisListType

B, N, D = 128, 64, 256
HEADS = 8
HD = D // HEADS
P = 128
EPS = 1e-5
ALPHA = 0.2
TILES = B * N // P
CT = 4
CW = CT * P
CHUNKS = TILES // CT
FT = D // P
BANK = 512
STEPS = 3
MASKED = -3e38


def wait(eng, sem, count):
    if not isinstance(count, int) or count > 0:
        eng.wait_ge(sem, count)


def wait_apart(eng, sem, count):
    if not isinstance(count, int):
        eng.wait_ge(sem, 1)
    eng.wait_ge(sem, count)


def exists(chunk):
    return not isinstance(chunk, int) or 0 <= chunk < CHUNKS


class Phase(ExitStack):

    def __init__(self, nc):
        super().__init__()
        self.handles = []
        self.callback(self.clear, nc)

    def semaphore(self, nc, name):
        self.handles.append(nc.alloc_semaphore(name))
        return self.handles[-1]

    def clear(self, nc):
        nc.clear_and_free_semaphores(self.handles)
        nc.all_engine_barrier()


def f32(ap):
    return ap.bitcast(F32)


class Parts:

    def __init__(self, ctx, nc, name, shape):
        self.hi = ctx.enter_context(nc.sbuf_tensor(name + "_hi", shape, F32R))
        self.lo = ctx.enter_context(nc.sbuf_tensor(name + "_lo", shape, F32R))


def product(pe, out, stationary, moving, begins=True, ends=True):
    terms = []
    for s, m in zip(stationary, moving):
        terms += [(s[0], m[0]), (s[0], m[1]), (s[1], m[0])]
    for n, (s, m) in enumerate(terms):
        last = pe.matmul(out, s, m, start=(begins and n == 0),
                         stop=(ends and n == len(terms) - 1))
    return last


def pair(parts, *index):
    return parts.hi[index], parts.lo[index]


def spread_rows(ap, times):
    return ap.rearrange("(a n) -> a n", a=1).to_broadcast([times, ap.shape[0]])


def load_columns(ap):
    return ap.rearrange("(f p) -> p f", p=P)


class LayerNorm:

    def __init__(self, nc, ctx, tag, x, ident, transposed=True):
        def sb(name, shape, dt=F32):
            return ctx.enter_context(nc.sbuf_tensor(f"{tag}_{name}", shape, dt))

        def sem(name):
            return ctx.semaphore(nc, f"{tag}_{name}")

        self.x, self.ident = x, ident
        self.stats = sb("stats", [P, CT, 6])
        self.mean_var = sb("mean_var", [P, CT, 2])
        self.var_eps = sb("var_eps", [P, CT])
        self.rstd = sb("rstd", [P, CT])
        self.minus_half = sb("minus_half", [P, CT])
        self.eps = sb("eps", [P, CT])
        self.carrier = sb("carrier", [P, 1])
        self.xn = sb("xn", [P, CT, D])
        if transposed:
            self.hT = Parts(ctx, nc, f"{tag}_hT", [P, FT, CW])
        self.bn_done = sem("bn_done")
        self.stats_ready = sem("stats_ready")
        self.half_ready = sem("half_ready")
        self.var_ready = sem("var_ready")
        self.rstd_ready = sem("rstd_ready")
        self.xn_ready = sem("xn_ready")
        self.xT_ready = sem("xT_ready")
        self.hT_hi_ready = sem("hT_hi_ready")
        self.hT_lo_ready = sem("hT_lo_ready")

    def dve_carry(self, dve, sem, count):
        dve.wait_ge(sem, count)
        dve.memset(self.carrier[:], 0.0)

    def dve_stats(self, dve, c):
        for t in range(CT):
            last = dve.bn_stats(self.stats[:, t, :], self.x[:, bass.ds(c * CT + t, 1), :])
        last.then_inc(self.bn_done, 1)
        self.dve_carry(dve, self.bn_done, c + 1)
        for t in range(CT):
            last = dve.bn_aggr(self.mean_var[:, t, :], self.stats[:, t, :])
        last.then_inc(self.stats_ready, 1)

    def pool_setup(self, pool):
        pool.memset(self.minus_half[:], -0.5).then_inc(self.half_ready, 1)
        pool.memset(self.eps[:], EPS).then_inc(self.half_ready, 1)
        pool.wait_ge(self.half_ready, 2)

    def pool_rstd(self, pool, c):
        pool.wait_ge(self.stats_ready, c + 1)
        pool.tensor_tensor(self.var_eps[:], self.mean_var[:, :, 1], self.eps[:], ALU.add)\
            .then_inc(self.var_ready, 1)
        pool.wait_ge(self.var_ready, c + 1)
        pool.tensor_tensor(self.rstd[:], self.var_eps[:], self.minus_half[:], ALU.pow)\
            .then_inc(self.rstd_ready, 1)

    def dve_normalise(self, dve, c):
        dve.wait_ge(self.rstd_ready, c + 1)
        wait(dve, self.xT_ready, c * FT)
        for t in range(CT):
            last = dve.tensor_scalar(self.xn[:, t:t + 1, :], self.x[:, bass.ds(c * CT + t, 1), :],
                                     self.mean_var[:, t, 0:1], self.rstd[:, t:t + 1],
                                     ALU.subtract, ALU.mult)
        last.then_inc(self.xn_ready, 1)

    def pe_transpose(self, pe, c, f, bank):
        pe.wait_ge(self.xn_ready, c + 1)
        for t in range(CT):
            last = pe.transpose(bank[:, t * P:(t + 1) * P], self.xn[:, t, f * P:(f + 1) * P], self.ident[:])
        last.then_inc(self.xT_ready, 1)

    def act_high(self, act, c, f, bank):
        act.wait_ge(self.xT_ready, c * FT + f + 1)
        act.activation(self.hT.hi[:, f, :], bank, ACT.Relu).then_inc(self.hT_hi_ready, 1)

    def dve_low(self, dve, c, f, bank):
        dve.wait_ge(self.hT_hi_ready, c * FT + f + 1)
        dve.scalar_tensor_tensor(self.hT.lo[:, f, :], bank, 0.0, f32(self.hT.hi[:, f, :]),
                                 ALU.max, ALU.subtract).then_inc(self.hT_lo_ready, 1)


def attention_phase(nc, tag, x, ident, psum, w, first_load=None, tail_norm=None):
    scores, ring = psum
    R = P // HD
    SCALE = float(np.float32(1.0) / np.sqrt(np.float32(HD)))
    BEGIN = 3
    with Phase(nc) as ctx:
        def sb(name, shape, dt=F32):
            return ctx.enter_context(nc.sbuf_tensor(f"{tag}_{name}", shape, dt))

        def sem(name):
            return ctx.semaphore(nc, f"{tag}_{name}")

        ln = LayerNorm(nc, ctx, tag, x, ident)
        hT = ln.hT
        names = ["q", "k", "v", "o"]
        parts = {n: Parts(ctx, nc, f"{tag}_w{n}", [P, FT, D]) for n in names}
        stage = sb("stage", [P, len(names), FT, D])
        mask = sb("mask", [P, N])
        adj2 = sb("adj2", [P, N])
        mask1 = sb("mask1", [P, N])
        out_bias = sb("out_bias", [P, D])
        col_bias = sb("col_bias", [P, 3, FT])
        qT = sb("qT", [P, FT, CW])
        kT = sb("kT", [P, FT, CW])
        v = sb("v", [P, 2, CT, 2, P])
        s = sb("s", [P, 2, R, CT, 2, N])
        mx = sb("mx", [P, R, CT * 2])
        total = sb("total", [P, R, CT * 2])
        rtotal = sb("rtotal", [P, R, CT * 2])
        pT = sb("pT", [P, R, CT, P])
        oT = Parts(ctx, nc, f"{tag}_oT", [P, FT, CW])
        if tail_norm:
            o = sb("o", [P, CT, D])
            o_n = sb("o_n", [P, CT, D])
            o_stats = sb("o_stats", [P, CT, 6])
            o_mv = sb("o_mv", [P, CT, 2])
            o_var = sb("o_var", [P, CT])
            o_rstd = sb("o_rstd", [P, CT])
            gamma = sb("gamma", [P, D])
            beta = sb("beta", [P, D])

        w_loaded = [sem(f"w{n}_loaded") for n in names]
        small_loaded = sem("small_loaded")
        w_hi_ready = sem("w_hi_ready")
        w_lo_ready = sem("w_lo_ready")
        mask_steps = sem("mask_steps")
        qk_ready = sem("qk_ready")
        qk_copied = sem("qk_copied")
        v_ready = sem("v_ready")
        v_copied = sem("v_copied")
        s_ready = sem("s_ready")
        s_masked = sem("s_masked")
        s_max = sem("s_max")
        s_shifted = sem("s_shifted")
        p_exp = sem("p_exp")
        p_total = sem("p_total")
        p_rtotal = sem("p_rtotal")
        p_ready = sem("p_ready")
        pT_ready = sem("pT_ready")
        pT_copied = sem("pT_copied")
        oT_ready = sem("oT_ready")
        oT_hi_ready = sem("oT_hi_ready")
        oT_lo_ready = sem("oT_lo_ready")
        out_ready = sem("out_ready")
        x_biased = sem("x_biased")
        x_done = sem("x_done")
        if tail_norm:
            o_bn = sem("o_bn")
            o_mv_ready = sem("o_mv_ready")
            o_var_ready = sem("o_var_ready")
            o_rstd_ready = sem("o_rstd_ready")
            o_n_ready = sem("o_n_ready")
            o_scaled = sem("o_scaled")
            o_ln_ready = sem("o_ln_ready")
            x_plus_o = sem("x_plus_o")
            x_final = sem("x_final")

        x_loaded = [sem(f"x_loaded{n}") for n in range(3)] if first_load is not None else None
        X_CUTS = [0, 1, 3, CHUNKS]

        small = [(adj2[0:N, :], w["adj"]), (adj2[N:P, :], w["adj"]), (out_bias[:], spread_rows(w["bo"], P))]
        if "bq" in w:
            small += [(col_bias[:, n, :], load_columns(w[b])) for n, b in enumerate(("bq", "bk", "bv"))]
        if tail_norm:
            small += [(gamma[:], spread_rows(tail_norm["gamma"], P)), (beta[:], spread_rows(tail_norm["beta"], P))]

        def iterations(eng, body, last):
            for i in range(-1, BEGIN):
                body(i, i % 2)
            with eng.Fori(0, (CHUNKS - 3 - BEGIN) // 2) as j:
                body(j * 2 + BEGIN, 1)
                body(j * 2 + BEGIN + 1, 0)
            for i in range(CHUNKS - 3, CHUNKS + last):
                body(i, i % 2)

        with nc.Block() as block:
            @block.sync
            def _(sp):
                if first_load is not None:
                    xs = first_load.rearrange("b n d -> (b n) d").rearrange("(t p) d -> p t d", p=P)
                    sp.dma_start(x[:, 0:CT, :], xs[:, 0:CT, :]).then_inc(x_loaded[0], 16)
                for n, name in enumerate(names[:3]):
                    sp.dma_start(stage[:, n, :, :], w["w" + name]).then_inc(w_loaded[n], 16)
                for dst, src in small:
                    sp.dma_start(dst, src).then_inc(small_loaded, 16)
                sp.dma_start(stage[:, 3, :, :], w["wo"]).then_inc(w_loaded[3], 16)
                if first_load is not None:
                    for n in (1, 2):
                        a, b = X_CUTS[n] * CT, X_CUTS[n + 1] * CT
                        sp.dma_start(x[:, a:b, :], xs[:, a:b, :]).then_inc(x_loaded[n], 16)

            @block.gpsimd
            def _(pool):
                ln.pool_setup(pool)
                if tail_norm:
                    pool.wait_ge(small_loaded, 16 * len(small))
                else:
                    pool.wait_ge(small_loaded, 16 * len(small))

                def shift(i, par, r):
                    pool.wait_ge(s_max, i * R + r + 1)
                    sr = s[:, par, r, :, :, :].rearrange("p t m k -> p (t m) k")
                    pool.tensor_tensor(sr, sr, mx[:, r, :].unsqueeze(2).to_broadcast([P, CT * 2, N]),
                                       ALU.subtract).then_inc(s_shifted, 1)

                def normalise(i, par, r):
                    pool.wait_ge(p_rtotal, i * R + r + 1)
                    sr = s[:, par, r, :, :, :].rearrange("p t m k -> p (t m) k")
                    pool.tensor_tensor(sr, sr, rtotal[:, r, :].unsqueeze(2).to_broadcast([P, CT * 2, N]),
                                       ALU.mult).then_inc(p_ready, 1)

                def body(i, par):
                    if isinstance(i, int) and i == -1:
                        ln.pool_rstd(pool, 0)
                        ln.pool_rstd(pool, 1)
                        return
                    if exists(i):
                        shift(i, par, 0)
                        shift(i, par, 1)
                        shift(i, par, 2)
                        shift(i, par, 3)
                    if tail_norm and exists(i - 3):
                        c = i - 3
                        pool.wait_ge(o_n_ready, c + 1)
                        pool.tensor_tensor(o_n[:], o_n[:], gamma[:].unsqueeze(1).to_broadcast([P, CT, D]),
                                           ALU.mult).then_inc(o_scaled, 1)
                        pool.wait_ge(o_scaled, c + 1)
                        pool.tensor_tensor(o_n[:], o_n[:], beta[:].unsqueeze(1).to_broadcast([P, CT, D]),
                                           ALU.add).then_inc(o_ln_ready, 1)
                    if exists(i):
                        normalise(i, par, 0)
                    if tail_norm and exists(i - 2):
                        c = i - 2
                        pool.wait_ge(o_mv_ready, c + 1)
                        pool.tensor_tensor(o_var[:], o_mv[:, :, 1], ln.eps[:], ALU.add)\
                            .then_inc(o_var_ready, 1)
                        pool.wait_ge(o_var_ready, c + 1)
                        pool.tensor_tensor(o_rstd[:], o_var[:], ln.minus_half[:], ALU.pow)\
                            .then_inc(o_rstd_ready, 1)
                    if exists(i + 2):
                        ln.pool_rstd(pool, i + 2)
                    if exists(i):
                        normalise(i, par, 1)
                        normalise(i, par, 2)
                    if not tail_norm and exists(i - 1):
                        pool.wait_ge(ln.xn_ready, i)
                        xc = x[:, bass.ds((i - 1) * CT, CT), :]
                        pool.tensor_tensor(xc, xc, out_bias[:].unsqueeze(1).to_broadcast([P, CT, D]),
                                           ALU.add).then_inc(x_biased, 1)
                    if tail_norm and exists(i - 2):
                        xc = x[:, bass.ds((i - 2) * CT, CT), :]
                        pool.tensor_tensor(xc, xc, o[:], ALU.add).then_inc(x_plus_o, 1)
                    if exists(i):
                        normalise(i, par, 3)

                iterations(pool, body, 3 if tail_norm else 1)

            @block.scalar
            def _(act):
                for n in range(len(names)):
                    act.wait_ge(w_loaded[n], 16)
                    act.activation(parts[names[n]].hi[:], stage[:, n, :, :], ACT.Copy).then_inc(w_hi_ready, 1)
                if "bq" in w:
                    act.wait_ge(small_loaded, 16 * len(small))

                def exponential(i, par, r):
                    act.wait_ge(s_shifted, i * R + r + 1)
                    sr = s[:, par, r, :, :, :]
                    act.activation(sr, sr, ACT.Exp).then_inc(p_exp, 1)

                def copy_v(i, par, g):
                    act.wait_ge(v_ready, i * 2 + g + 1)
                    vb = ring[:, 2 + g, :].rearrange("p (t c) -> p t c", t=2)
                    for m in range(2):
                        for gr in range(2):
                            last = act.activation(
                                v[m * N:(m + 1) * N, par, 2 * g:2 * g + 2, gr, :],
                                vb[gr * N:(gr + 1) * N, :, m * P:(m + 1) * P], ACT.Copy)
                    last.then_inc(v_copied, 1)

                def body(i, par):
                    if exists(i):
                        exponential(i, par, 0)
                        copy_v(i, par, 0)
                        exponential(i, par, 1)
                        copy_v(i, par, 1)
                    if exists(i - 1):
                        for r in range(R):
                            act.wait_ge(pT_ready, (i - 1) * R + r + 1)
                            act.activation(pT[:, r, :, :].rearrange("p t q -> p (t q)"), ring[:, r, :],
                                           ACT.Copy).then_inc(pT_copied, 1)
                    if exists(i + 1):
                        for f in range(FT):
                            ln.act_high(act, i + 1, f, ring[:, f, :])
                    if exists(i):
                        exponential(i, par, 2)
                        exponential(i, par, 3)
                    if exists(i - 1):
                        for m in range(FT):
                            act.wait_ge(oT_ready, (i - 1) * FT + m + 1)
                            if "bq" in w:
                                ins = act.activation(oT.hi[:, m, :], ring[:, 2 + m, :], ACT.Identity,
                                                     bias=col_bias[:, 2, m:m + 1])
                            else:
                                ins = act.activation(oT.hi[:, m, :], ring[:, 2 + m, :], ACT.Copy)
                            ins.then_inc(oT_hi_ready, 1)
                    if exists(i + 1):
                        c = i + 1
                        for n, dst in enumerate((qT, kT)):
                            for m in range(FT):
                                act.wait_ge(qk_ready, c * 2 * FT + n * FT + m + 1)
                                if "bq" in w:
                                    ins = act.activation(dst[:, m, :], ring[:, 2 * n + m, :], ACT.Identity,
                                                         bias=col_bias[:, n, m:m + 1])
                                else:
                                    ins = act.activation(dst[:, m, :], ring[:, 2 * n + m, :], ACT.Copy)
                                ins.then_inc(qk_copied, 1)

                iterations(act, body, 1)

            @block.vector
            def _(dve):
                def chunk_loaded(c):
                    if first_load is not None and isinstance(c, int) and c in X_CUTS:
                        dve.wait_ge(x_loaded[X_CUTS.index(c)], 16)

                chunk_loaded(0)
                ln.dve_stats(dve, 0)
                for n in range(len(names)):
                    dve.wait_ge(w_hi_ready, n + 1)
                    dve.tensor_tensor(parts[names[n]].lo[:], stage[:, n, :, :], f32(parts[names[n]].hi[:]),
                                      ALU.subtract).then_inc(w_lo_ready, 1)
                    if n == 0:
                        ln.dve_normalise(dve, 0)
                        dve.wait_ge(small_loaded, 16 * len(small))
                        if w["fill"] == "additive":
                            dve.tensor_scalar(mask1[:], adj2[:], -1.0, 1.0, ALU.mult, ALU.add)\
                                .then_inc(mask_steps, 1)
                            dve.wait_ge(mask_steps, 1)
                            dve.tensor_scalar(mask[:], mask1[:], -1e9, None, ALU.mult)\
                                .then_inc(mask_steps, 1)
                        else:
                            dve.tensor_scalar(mask[:], adj2[:], 0.0, MASKED, ALU.is_equal, ALU.mult)\
                                .then_inc(mask_steps, 2)
                        dve.wait_ge(mask_steps, 2)

                def sr(par, r):
                    return s[:, par, r, :, :, :].rearrange("p t m k -> p (t m) k")

                def mask_and_max(i, par, r):
                    dve.wait_ge(s_ready, i * R + r + 1)
                    dve.scalar_tensor_tensor(
                        sr(par, r), scores[:, r, :].rearrange("p (a k) -> p a k", k=N), SCALE,
                        mask[:].unsqueeze(1).to_broadcast([P, CT * 2, N]),
                        ALU.mult, ALU.add).then_inc(s_masked, 1)
                    dve.wait_ge(s_masked, i * R + r + 1)
                    dve.reduce_max(mx[:, r, :], sr(par, r), AX.X).then_inc(s_max, 1)

                def sums(i, par, r):
                    dve.wait_ge(p_exp, i * R + r + 1)
                    dve.reduce_sum(total[:, r, :], sr(par, r), AX.X).then_inc(p_total, 1)
                    dve.wait_ge(p_total, i * R + r + 1)
                    dve.reciprocal(rtotal[:, r, :], total[:, r, :]).then_inc(p_rtotal, 1)

                def take_out(c, g):
                    dve.wait_ge(out_ready, c * 2 + g + 1)
                    ob = ring[:, g, :].rearrange("p (t c) -> p t c", t=2)
                    if tail_norm:
                        dve.tensor_tensor(o[:, 2 * g:2 * g + 2, :], ob,
                                          out_bias[:].unsqueeze(1).to_broadcast([P, 2, D]),
                                          ALU.add).then_inc(x_done, 1)
                    else:
                        xc = x[:, bass.ds(c * CT + 2 * g, 2), :]
                        dve.tensor_tensor(xc, xc, ob, ALU.add).then_inc(x_done, 1)

                def body(i, par):
                    if isinstance(i, int) and i == -1:
                        for f in range(FT):
                            ln.dve_low(dve, 0, f, ring[:, f, :])
                        chunk_loaded(1)
                        ln.dve_stats(dve, 1)
                        ln.dve_normalise(dve, 1)
                        return
                    if isinstance(i, int) and i == 0 and first_load is not None:
                        dve.wait_ge(x_loaded[2], 16)
                    if exists(i - 2):
                        c = i - 2
                        if not tail_norm:
                            dve.wait_ge(x_biased, c + 1)
                        else:
                            wait(dve, x_plus_o, c)
                            wait(dve, o_n_ready, c)
                        take_out(c, 0)
                    if exists(i):
                        mask_and_max(i, par, 0)
                    if exists(i - 2):
                        take_out(i - 2, 1)
                    if exists(i):
                        mask_and_max(i, par, 1)
                    if tail_norm and exists(i - 2):
                        c = i - 2
                        dve.wait_ge(x_done, c * 2 + 2)
                        for t in range(CT):
                            last = dve.bn_stats(o_stats[:, t, :], o[:, t, :])
                        last.then_inc(o_bn, 1)
                        ln.dve_carry(dve, o_bn, c + 1)
                        for t in range(CT):
                            last = dve.bn_aggr(o_mv[:, t, :], o_stats[:, t, :])
                        last.then_inc(o_mv_ready, 1)
                    if exists(i):
                        mask_and_max(i, par, 2)
                    if exists(i):
                        mask_and_max(i, par, 3)
                    if exists(i + 1):
                        for f in range(FT):
                            ln.dve_low(dve, i + 1, f, ring[:, f, :])
                    if exists(i + 2):
                        ln.dve_stats(dve, i + 2)
                    if exists(i):
                        sums(i, par, 0)
                    if exists(i - 1):
                        c = i - 1
                        for m in range(FT):
                            dve.wait_ge(oT_hi_ready, c * FT + m + 1)
                            if "bq" in w:
                                ins = dve.scalar_tensor_tensor(oT.lo[:, m, :], ring[:, 2 + m, :],
                                                               col_bias[:, 2, m:m + 1], f32(oT.hi[:, m, :]),
                                                               ALU.add, ALU.subtract)
                            else:
                                ins = dve.tensor_tensor(oT.lo[:, m, :], ring[:, 2 + m, :],
                                                        f32(oT.hi[:, m, :]), ALU.subtract)
                            ins.then_inc(oT_lo_ready, 1)
                    if exists(i):
                        for r in range(1, R):
                            sums(i, par, r)
                    if tail_norm and exists(i - 3):
                        c = i - 3
                        dve.wait_ge(o_ln_ready, c + 1)
                        dve.wait_ge(x_plus_o, c + 1)
                        xc = x[:, bass.ds(c * CT, CT), :]
                        dve.tensor_tensor(xc, xc, o_n[:], ALU.add).then_inc(x_final, 1)
                    if tail_norm and exists(i - 2):
                        c = i - 2
                        dve.wait_ge(o_rstd_ready, c + 1)
                        wait(dve, x_final, c)
                        for t in range(CT):
                            last = dve.tensor_scalar(o_n[:, t, :], o[:, t, :], o_mv[:, t, 0:1],
                                                     o_rstd[:, t:t + 1], ALU.subtract, ALU.mult)
                        last.then_inc(o_n_ready, 1)
                    if exists(i + 2):
                        ln.dve_normalise(dve, i + 2)

                iterations(dve, body, 3 if tail_norm else 2)

            @block.tensor
            def _(pe):
                def columns(parts_, m):
                    return [pair(parts_, slice(None), k, slice(m * P, (m + 1) * P)) for k in range(FT)]

                hT_moving = [pair(hT, slice(None), k, slice(None)) for k in range(FT)]

                def scores_of(i, r):
                    rows = slice(r * HD, (r + 1) * HD)
                    for t in range(CT):
                        for m in range(2):
                            for g in range(2):
                                tok = slice(t * P + g * N, t * P + (g + 1) * N)
                                last = pe.matmul(
                                    scores[g * N:(g + 1) * N, r, (2 * t + m) * N:(2 * t + m + 1) * N],
                                    qT[rows, m, tok], kT[rows, m, tok], start=True, stop=True)
                    last.then_inc(s_ready, 1)

                def rows_product(stationary, weight, bank, g, signal):
                    for t in (2 * g, 2 * g + 1):
                        stat = [pair(stationary, slice(None), k, slice(t * P, (t + 1) * P)) for k in range(FT)]
                        mov = [pair(weight, slice(None), k, slice(None)) for k in range(FT)]
                        last = product(pe, ring[:, bank, (t % 2) * D:(t % 2 + 1) * D], stat, mov)
                    last.then_inc(signal, 1)

                def body(i, par):
                    if exists(i - 2):
                        if exists(i):
                            pe.wait_ge(qk_copied, i * 2 * FT + FT)
                        pe.wait_ge(oT_lo_ready, (i - 1) * FT)
                        rows_product(oT, parts["o"], 0, 0, out_ready)
                    if exists(i):
                        pe.wait_ge(qk_copied, (i + 1) * 2 * FT)
                        wait(pe, s_masked, i * R)
                        scores_of(i, 0)
                    if exists(i - 2):
                        rows_product(oT, parts["o"], 1, 1, out_ready)
                    if exists(i):
                        scores_of(i, 1)
                        if isinstance(i, int) and i == 0:
                            pe.wait_ge(w_lo_ready, 4)
                        rows_product(hT, parts["v"], 2, 0, v_ready)
                        scores_of(i, 2)
                        rows_product(hT, parts["v"], 3, 1, v_ready)
                        scores_of(i, 3)
                    if exists(i - 1):
                        c = i - 1
                        for r in range(R):
                            if r < 2:
                                wait(pe, x_done, (i - 2) * 2 + r + 1)
                            elif exists(i):
                                pe.wait_ge(v_copied, i * 2 + r - 1)
                            pe.wait_ge(p_ready, c * R + r + 1)
                            for t in range(CT):
                                last = pe.transpose(
                                    ring[:, r, t * P:(t + 1) * P],
                                    s[:, 1 - par, r, t, :, :].rearrange("p m k -> p (m k)"), ident[:])
                            last.then_inc(pT_ready, 1)
                    if exists(i + 1):
                        for f in range(FT):
                            if exists(i - 1):
                                pe.wait_ge(pT_copied, (i - 1) * R + f + 1)
                            ln.pe_transpose(pe, i + 1, f, ring[:, f, :])
                    if exists(i - 1):
                        c = i - 1
                        wait_apart(pe, pT_copied, i * R)
                        for m in range(FT):
                            rows = slice(m * N, (m + 1) * N)
                            for t in range(CT):
                                for g in range(2):
                                    for r in range(R):
                                        tok = slice(t * P + g * N, t * P + (g + 1) * N)
                                        last = pe.matmul(
                                            ring[r * HD:(r + 1) * HD, 2 + m, tok],
                                            v[rows, 1 - par, t, g, r * HD:(r + 1) * HD],
                                            pT[rows, r, t, g * N:(g + 1) * N], start=True, stop=True)
                            last.then_inc(oT_ready, 1)
                    if exists(i + 1):
                        c = i + 1
                        for n, name in enumerate(("q", "k")):
                            if isinstance(i, int) and i == -1:
                                pe.wait_ge(w_lo_ready, n + 1)
                            if n == 0:
                                pe.wait_ge(ln.hT_lo_ready, FT * (c + 1))
                            elif isinstance(i, int) and i == 0:
                                pe.wait_ge(v_copied, 2)
                            for m in range(FT):
                                if n == 1 and exists(i - 1):
                                    pe.wait_ge(oT_lo_ready, (i - 1) * FT + m + 1)
                                product(pe, ring[:, 2 * n + m, :], columns(parts[name], m), hT_moving)\
                                    .then_inc(qk_ready, 1)

                iterations(pe, body, 2)


def graph_attention_phase(nc, x, ident, psum, a, next_weights):
    wide, ring = psum
    WX = D + 2
    with Phase(nc) as ctx:
        def sb(name, shape, dt=F32):
            return ctx.enter_context(nc.sbuf_tensor(f"l2_{name}", shape, dt))

        def sem(name):
            return ctx.semaphore(nc, f"l2_{name}")

        ln = LayerNorm(nc, ctx, "l2", x, ident)
        hT = ln.hT
        w_ext = sb("w_ext", [P, FT, WX])
        w = Parts(ctx, nc, "l2_w", [P, FT, WX])
        wa2 = Parts(ctx, nc, "l2_wa2", [P, FT, P])
        a_rows = sb("a_rows", [P, 2, D])
        wa_terms = sb("wa_terms", [P, 2, FT, D])
        adj2 = sb("adj2", [P, N])
        beta = sb("beta", [P, 1])
        hw = sb("hw", [P, 2, CT, WX])
        e = sb("e", [P, CT, N])
        e_lrelu = sb("e_lrelu", [P, CT, N])
        mx = sb("mx", [P, CT])
        total = sb("total", [P, CT])
        rtotal = sb("rtotal", [P, CT])
        att = sb("att", [P, CT, 2, N])
        attT = sb("attT", [P, CT, P])
        beta_ident = sb("beta_ident", [P, P])
        y_neg = sb("y_neg", [P, CT, D])
        y_pos = sb("y_pos", [P, CT, D])

        w_loaded = sem("w_loaded")
        small_loaded = sem("small_loaded")
        wa_steps = sem("wa_steps")
        w_hi_ready = sem("w_hi_ready")
        w_lo_ready = sem("w_lo_ready")
        att_cleared = sem("att_cleared")
        s2_ready = sem("s2_ready")
        hw_ready = sem("hw_ready")
        hw_copied = sem("hw_copied")
        e_sum = sem("e_sum")
        e_leaky = sem("e_leaky")
        e_masked = sem("e_masked")
        e_max = sem("e_max")
        e_shifted = sem("e_shifted")
        e_exp = sem("e_exp")
        e_total = sem("e_total")
        e_rtotal = sem("e_rtotal")
        att_ready = sem("att_ready")
        attT_ready = sem("attT_ready")
        attT_copied = sem("attT_copied")
        beta_ident_ready = sem("beta_ident_ready")
        agg_ready = sem("agg_ready")
        y_read = sem("y_read")
        y_exp_ready = sem("y_exp_ready")
        x_plus_pos = sem("x_plus_pos")
        x_done = sem("x_done")

        BEGIN = 3

        def iterations(eng, body):
            for i in range(-1, BEGIN):
                body(i, i % 2)
            with eng.Fori(0, (CHUNKS - 3 - BEGIN) // 2) as j:
                body(j * 2 + BEGIN, 1)
                body(j * 2 + BEGIN + 1, 0)
            for i in range(CHUNKS - 3, CHUNKS + 1):
                body(i, i % 2)

        with nc.Block() as block:
            @block.sync
            def _(sp):
                sp.dma_start(w_ext[:, :, 0:D], a["L2_gnn_W"].rearrange("(k p) n -> p k n", p=P)).then_inc(w_loaded, 16)
                for n in range(2):
                    row = a["L2_gnn_a"][n * D:(n + 1) * D, :].rearrange("n a -> (n a)")
                    sp.dma_start(a_rows[:, n, :], spread_rows(row, P)).then_inc(small_loaded, 16)
                for g in range(2):
                    sp.dma_start(adj2[g * N:(g + 1) * N, :], a["adj"]).then_inc(small_loaded, 16)
                sp.dma_start(beta[:], spread_rows(a["L2_gnn_beta"], P)).then_inc(small_loaded, 16)
                next_weights.load(sp)

            @block.gpsimd
            def _(pool):
                ln.pool_setup(pool)
                pool.memset(att[:], 0.0).then_inc(att_cleared, 1)
                pool.wait_ge(att_cleared, 1)

                def body(i, par):
                    if isinstance(i, int) and i == -1:
                        ln.pool_rstd(pool, 0)
                        ln.pool_rstd(pool, 1)
                        return
                    if exists(i):
                        pool.wait_ge(e_max, i + 1)
                        pool.tensor_tensor(e[:], e[:], mx[:].unsqueeze(2).to_broadcast([P, CT, N]),
                                           ALU.subtract).then_inc(e_shifted, 1)
                    if exists(i + 2):
                        ln.pool_rstd(pool, i + 2)
                    if exists(i - 1):
                        c = i - 1
                        pool.wait_ge(y_read, (c + 1) * 2)
                        xc = x[:, bass.ds(c * CT, CT), :]
                        pool.tensor_tensor(xc, xc, y_pos[:], ALU.add).then_inc(x_plus_pos, 1)

                iterations(pool, body)

            @block.scalar
            def _(act):
                act.wait_ge(wa_steps, 2)
                act.activation(w.hi[:], w_ext[:], ACT.Copy).then_inc(w_hi_ready, 1)
                act.activation(wa2.hi[:], w_ext[:, :, D + 1:D + 2].to_broadcast([P, FT, P]), ACT.Copy)\
                    .then_inc(w_hi_ready, 1)

                def copy_hw(i, par, t):
                    act.wait_ge(hw_ready, i * CT + t + 1)
                    act.activation(hw[:, par, t, :], wide[:, t, 0:WX], ACT.Copy).then_inc(hw_copied, 1)

                def body(i, par):
                    if exists(i + 1):
                        for f in range(FT):
                            ln.act_high(act, i + 1, f, ring[:, f, :])
                    if exists(i - 1):
                        c = i - 1
                        wait(act, x_done, c)
                        for g in range(2):
                            act.wait_ge(agg_ready, c * 2 + g + 1)
                            y = wide[:, 2 + g, 0:2 * D].rearrange("p (t c) -> p t c", t=2)
                            tiles = slice(2 * g, 2 * g + 2)
                            act.activation(y_pos[:, tiles, :], y, ACT.Relu)
                            act.activation(y_neg[:, tiles, :], y, ACT.Relu, scale=-1.0).then_inc(y_read, 1)
                        act.wait_ge(y_read, (c + 1) * 2)
                        act.activation(y_neg[:], y_neg[:], ACT.Exp, scale=-1.0).then_inc(y_exp_ready, 1)
                    if exists(i + 1):
                        for t in (0, 1):
                            copy_hw(i + 1, 1 - par, t)
                    if exists(i):
                        act.wait_ge(e_shifted, i + 1)
                        act.activation(e[:], e[:], ACT.Exp).then_inc(e_exp, 1)
                    if exists(i + 1):
                        for t in (2, 3):
                            copy_hw(i + 1, 1 - par, t)

                iterations(act, body)

            @block.vector
            def _(dve):
                ln.dve_stats(dve, 0)
                ln.dve_normalise(dve, 0)
                dve.wait_ge(att_cleared, 1)
                dve.wait_ge(w_loaded, 16)
                dve.wait_ge(small_loaded, 16 * 5)
                for n in range(2):
                    last = dve.tensor_tensor(wa_terms[:, n, :, :], w_ext[:, :, 0:D],
                                             a_rows[:, n, :].unsqueeze(1).to_broadcast([P, FT, D]), ALU.mult)
                last.then_inc(wa_steps, 1)
                dve.wait_ge(wa_steps, 1)
                for n in range(2):
                    last = dve.reduce_sum(w_ext[:, :, D + n], wa_terms[:, n, :, :], AX.X)
                last.then_inc(wa_steps, 1)
                dve.wait_ge(w_hi_ready, 1)
                dve.tensor_tensor(w.lo[:], w_ext[:], f32(w.hi[:]), ALU.subtract).then_inc(w_lo_ready, 1)
                dve.wait_ge(w_hi_ready, 2)
                dve.tensor_tensor(wa2.lo[:], w_ext[:, :, D + 1:D + 2].to_broadcast([P, FT, P]), f32(wa2.hi[:]),
                                  ALU.subtract).then_inc(w_lo_ready, 1)

                dve.tensor_scalar(beta_ident[:], ident[:], beta[:, 0:1], None, ALU.mult).then_inc(beta_ident_ready, 1)
                dve.wait_ge(beta_ident_ready, 1)

                def body(i, par):
                    if exists(i + 1):
                        for f in range(FT):
                            ln.dve_low(dve, i + 1, f, ring[:, f, :])
                    if isinstance(i, int) and i == -1:
                        ln.dve_stats(dve, 1)
                        ln.dve_normalise(dve, 1)
                        return
                    if exists(i):
                        dve.wait_ge(s2_ready, i + 1)
                        dve.wait_ge(hw_copied, (i + 1) * CT)
                        for g in range(2):
                            rows = slice(g * N, (g + 1) * N)
                            s2 = ring[rows, 2, :].rearrange("p (t g j) -> p t g j", g=2, j=N)[:, :, g, :]
                            last = dve.tensor_tensor(e[rows, :, :], s2,
                                                     hw[rows, par, :, D:D + 1].to_broadcast([N, CT, N]), ALU.add)
                        last.then_inc(e_sum, 1)
                        dve.wait_ge(e_sum, i + 1)
                        dve.scalar_tensor_tensor(e_lrelu[:], e[:], ALPHA, e[:], ALU.mult, ALU.max).then_inc(e_leaky, 1)
                        dve.wait_ge(e_leaky, i + 1)
                        dve.tensor_tensor(e[:], e_lrelu[:], adj2[:].unsqueeze(1).to_broadcast([P, CT, N]), ALU.mult)\
                            .then_inc(e_masked, 1)
                        dve.wait_ge(e_masked, i + 1)
                        dve.reduce_max(mx[:], e[:], AX.X).then_inc(e_max, 1)
                    if exists(i + 2):
                        ln.dve_stats(dve, i + 2)
                    if exists(i):
                        dve.wait_ge(e_exp, i + 1)
                        dve.reduce_sum(total[:], e[:], AX.X).then_inc(e_total, 1)
                        dve.wait_ge(e_total, i + 1)
                        dve.reciprocal(rtotal[:], total[:]).then_inc(e_rtotal, 1)
                        dve.wait_ge(e_rtotal, i + 1)
                        wait(dve, attT_ready, i)
                        for g in range(2):
                            rows = slice(g * N, (g + 1) * N)
                            last = dve.tensor_tensor(att[rows, :, g, :], e[rows, :, :],
                                                     rtotal[rows, :].unsqueeze(2).to_broadcast([N, CT, N]), ALU.mult)
                        last.then_inc(att_ready, 1)
                    if exists(i + 2):
                        ln.dve_normalise(dve, i + 2)
                    if exists(i):
                        wait(dve, agg_ready, i * 2)
                        dve.wait_ge(attT_ready, i + 1)
                        dve.tensor_tensor(attT[:], ring[:, 3, :].rearrange("p (t q) -> p t q", q=P),
                                          beta_ident[:].unsqueeze(1).to_broadcast([P, CT, P]), ALU.add)\
                            .then_inc(attT_copied, 1)
                    if exists(i - 1):
                        c = i - 1
                        dve.wait_ge(y_exp_ready, c + 1)
                        dve.wait_ge(x_plus_pos, c + 1)
                        xc = x[:, bass.ds(c * CT, CT), :]
                        dve.scalar_tensor_tensor(xc, y_neg[:], -1.0, xc, ALU.add, ALU.add).then_inc(x_done, 1)

                iterations(dve, body)

            @block.tensor
            def _(pe):
                hT_moving = [pair(hT, slice(None), k, slice(None)) for k in range(FT)]

                for f in range(FT):
                    ln.pe_transpose(pe, 0, f, ring[:, f, :])

                def body(i, par):
                    if exists(i + 1):
                        c = i + 1
                        if isinstance(i, int) and i == -1:
                            pe.wait_ge(w_lo_ready, 2)
                        pe.wait_ge(ln.hT_lo_ready, (c + 1) * FT)
                        for t in range(CT):
                            if exists(i - 1) and t >= 2:
                                pe.wait_ge(y_read, (i - 1) * 2 + t - 1)
                            stat = [pair(hT, slice(None), k, slice(t * P, (t + 1) * P)) for k in range(FT)]
                            mov = [pair(w, slice(None), k, slice(None)) for k in range(FT)]
                            product(pe, wide[:, t, 0:WX], stat, mov).then_inc(hw_ready, 1)
                        wait(pe, e_sum, c)
                        product(pe, ring[:, 2, :], [pair(wa2, slice(None), k, slice(None)) for k in range(FT)],
                                hT_moving).then_inc(s2_ready, 1)
                    if exists(i):
                        pe.wait_ge(att_ready, i + 1)
                        for t in range(CT):
                            last = pe.transpose(ring[:, 3, t * P:(t + 1) * P],
                                                att[:, t, :, :].rearrange("p g j -> p (g j)"), ident[:])
                        last.then_inc(attT_ready, 1)
                    if exists(i + 2):
                        for f in range(FT):
                            ln.pe_transpose(pe, i + 2, f, ring[:, f, :])
                    if exists(i):
                        if exists(i + 1):
                            pe.wait_ge(hw_copied, (i + 2) * CT)
                        else:
                            pe.wait_ge(y_read, i * 2)
                        pe.wait_ge(attT_copied, i + 1)
                        for g in range(2):
                            for t in (2 * g, 2 * g + 1):
                                last = pe.matmul(wide[:, 2 + g, (t % 2) * D:(t % 2 + 1) * D], attT[:, t, :],
                                                 hw[:, par, t, 0:D], start=True, stop=True)
                            last.then_inc(agg_ready, 1)

                iterations(pe, body)


class RecurrenceWeights:

    def __init__(self, nc, ctx, a):
        self.w = ctx.enter_context(nc.sbuf_tensor("l3_w_stage", [P, 3, FT, 2 * D], F32))
        self.u = ctx.enter_context(nc.sbuf_tensor("l3_u_stage", [P, 2, FT, D], F32))
        self.b = ctx.enter_context(nc.sbuf_tensor("l3_b_stage", [P, 5, FT], F32))
        self.w_loaded = ctx.enter_context(nc.semaphore("l3_w_loaded"))
        self.b_loaded = ctx.enter_context(nc.semaphore("l3_b_loaded"))
        self.a = a

    def load(self, sp):
        for n, m in enumerate(("w3", "w4", "w5")):
            sp.dma_start(self.w[:, n, :, :], self.a[f"L3_gnn_{m}_w"].rearrange("(o p) i -> p o i", p=P))\
                .then_inc(self.w_loaded, 16)
        for n, m in enumerate(("u3", "u5")):
            sp.dma_start(self.u[:, n, :, :], self.a[f"L3_gnn_{m}_w"].rearrange("(o p) i -> p o i", p=P))\
                .then_inc(self.w_loaded, 16)
        for n, m in enumerate(("w3", "w4", "w5", "u3", "u5")):
            sp.dma_start(self.b[:, n, :], load_columns(self.a[f"L3_gnn_{m}_b"])).then_inc(self.b_loaded, 16)


def recurrence_phase(nc, x, ident, psum, a, weights, out):
    bank_a, bank_b = psum
    ring, high = bank_b, bank_a
    GROUPS = CHUNKS // 2
    HALVES = 2 * STEPS
    with Phase(nc) as ctx:
        def sb(name, shape, dt=F32):
            return ctx.enter_context(nc.sbuf_tensor(f"l3_{name}", shape, dt))

        def sem(name):
            return ctx.semaphore(nc, f"l3_{name}")

        ln = LayerNorm(nc, ctx, "l3", x, ident, transposed=False)
        mats = ["w3", "w4", "w5", "u3", "u5"]
        wT = {m: Parts(ctx, nc, f"l3_{m}", [P, FT, D]) for m in mats}
        w_stage, u_stage, b_stage = weights.w, weights.u, weights.b
        bias = sb("bias", [P, 3, FT])
        adjT = sb("adjT", [P, P])
        adj = Parts(ctx, nc, "l3_adj", [P, P])
        h0 = [sb(f"h0_{q}", [P, FT, CW]) for q in "ab"]
        h = [sb(f"h_{q}", [P, FT, CW]) for q in "ab"]
        hp = [Parts(ctx, nc, f"l3_hp_{q}", [P, FT, CW]) for q in "ab"]
        tok = Parts(ctx, nc, "l3_tok", [P, CT, D])
        agg = Parts(ctx, nc, "l3_agg", [P, FT, CW])
        hu = sb("hu", [P, FT, CW])
        r = sb("r", [P, FT, CW])
        z = sb("z", [P, FT, CW])
        hv = sb("hv", [P, FT, CW])
        rh = sb("rh", [P, FT, CW])
        rhp = Parts(ctx, nc, "l3_rhp", [P, FT, CW])

        adj_cleared = sem("adj_cleared")
        adj_loaded = sem("adj_loaded")
        w_loaded, b_loaded = weights.w_loaded, weights.b_loaded
        halves_added = sem("halves_added")
        b_ready = sem("b_ready")
        wT_ready = sem("wT_ready")
        wT_hi_ready = sem("wT_hi_ready")
        wT_lo_ready = sem("wT_lo_ready")
        tok_ready = sem("tok_ready")
        tok_hi_ready = sem("tok_hi_ready")
        tok_lo_ready = sem("tok_lo_ready")
        hu_ready = sem("hu_ready")
        hu_copied = sem("hu_copied")
        agg_ready = sem("agg_ready")
        agg_hi_ready = sem("agg_hi_ready")
        agg_lo_ready = sem("agg_lo_ready")
        r_ready = sem("r_ready")
        r_added = sem("r_added")
        r_done = sem("r_done")
        z_ready = sem("z_ready")
        z_added = sem("z_added")
        z_done = sem("z_done")
        rh_done = sem("rh_done")
        rh_hi_ready = sem("rh_hi_ready")
        rh_lo_ready = sem("rh_lo_ready")
        hv_ready = sem("hv_ready")
        hv_done = sem("hv_done")
        hv_minus_h = sem("hv_minus_h")
        hv_gated = sem("hv_gated")
        h_done = sem("h_done")
        h_hi_ready = sem("h_hi_ready")
        h_lo_ready = sem("h_lo_ready")
        h0_hi_ready = sem("h0_hi_ready")
        h0_lo_ready = sem("h0_lo_ready")
        final_ready = sem("final_ready")
        x_done = sem("x_done")
        stored = sem("stored")

        class Half:

            def __init__(self, g, k):
                fixed = isinstance(g, int)
                self.n = g * HALVES + k
                self.k = k % HALVES
                self.first = fixed and self.n == 0
                self.last = fixed and self.n == GROUPS * HALVES
                self.step = self.k // 2
                self.stops = fixed and g == GROUPS - 1
                self.me = self.k % 2
                self.other = 1 - self.me
                group = g + 1 if k == HALVES else g
                self.chunk = group * 2 + self.me
                self.enters = self.leaves = self.left = None
                if self.k == HALVES - 1:
                    if not (fixed and group == GROUPS - 1):
                        self.enters = group * 2 + 2
                    self.leaves = group * 2
                if self.k == 0:
                    if not self.last:
                        self.enters = group * 2 + 1
                    if not self.first:
                        self.leaves = group * 2 - 1
                if self.k == 0 and not self.first:
                    self.left = group * 2 - 2
                self.later = group * (HALVES - 2) + self.k
                self.before_step = STEPS - 1 if self.k == 0 else (self.k - 1) // 2
                self.before_later = self.later

            def h_me(self):
                return h0[self.me] if self.step == 0 else h[self.me]

            def h_before(self):
                return h0[self.other] if self.before_step == 0 else h[self.other]

        def halves(eng, body):
            body(Half(0, 0))
            with eng.Fori(0, GROUPS - 1) as g:
                for k in range(1, HALVES + 1):
                    body(Half(g, k))
            for k in range(1, HALVES + 1):
                body(Half(GROUPS - 1, k))

        with nc.Block() as block:
            @block.sync
            def _(sp):
                sp.wait_ge(adj_cleared, 1)
                for g in range(2):
                    sp.dma_start(adjT[g * N:(g + 1) * N, g * N:(g + 1) * N], a["adj"].rearrange("i j -> j i"))\
                        .then_inc(adj_loaded, 16)
                dst = out.rearrange("b n d -> (b n) d").rearrange("(t p) d -> p t d", p=P)
                with sp.Fori(0, CHUNKS) as c:
                    sp.wait_ge(x_done, c * 2 + 2)
                    sp.dma_start(dst[:, bass.ds(c * CT, CT), :], x[:, bass.ds(c * CT, CT), :]).then_inc(stored, 16)
                sp.wait_ge(stored, 16 * CHUNKS)

            @block.gpsimd
            def _(pool):
                ln.pool_setup(pool)
                pool.memset(adjT[:], 0.0).then_inc(adj_cleared, 1)
                ln.pool_rstd(pool, 0)
                with pool.Fori(1, CHUNKS) as c:
                    ln.pool_rstd(pool, c)

            @block.scalar
            def _(act):
                for n, m in enumerate(mats):
                    act.wait_ge(wT_ready, n + 1)
                    bank = ring[:, n, :] if n < 4 else high[:, 0, :]
                    act.activation(wT[m].hi[:], bank.rearrange("p (k o) -> p k o", k=FT), ACT.Copy)\
                        .then_inc(wT_hi_ready, 1)
                act.wait_ge(adj_loaded, 32)
                act.activation(adj.hi[:], adjT[:], ACT.Copy).then_inc(wT_hi_ready, 1)
                act.wait_ge(b_ready, 3)

                def enter(c, me):
                    for f in range(FT):
                        act.wait_ge(ln.xT_ready, c * FT + f + 1)
                        act.activation(hp[me].hi[:, f, :], ring[:, 2 + f, :], ACT.Relu)
                        act.activation(h0[me][:, f, :], ring[:, 2 + f, :], ACT.Relu).then_inc(h0_hi_ready, 1)

                def body(s):
                    n = s.n
                    if not s.last:
                        for q in range(2):
                            act.wait_ge(tok_ready, n * 2 + q + 1)
                            act.activation(tok.hi[:, 2 * q:2 * q + 2, :],
                                           ring[:, q, :].rearrange("p (t d) -> p t d", t=2), ACT.Copy)\
                                .then_inc(tok_hi_ready, 1)
                    if not s.first:
                        for m in range(FT):
                            act.wait_ge(z_added, (n - 1) * FT + m + 1)
                            act.activation(z[:, m, :], z[:, m, :], ACT.Sigmoid, bias=bias[:, 0, m:m + 1])\
                                .then_inc(z_done, 1)
                    if not s.last:
                        act.wait_ge(hu_ready, n * FT + 1)
                        act.activation(hu[:, 0, :], ring[:, 2, :], ACT.Copy).then_inc(hu_copied, 1)
                    if not s.first:
                        act.wait_ge(rh_done, n)
                        act.activation(rhp.hi[:], rh[:], ACT.Copy).then_inc(rh_hi_ready, 1)
                    if not s.last:
                        act.wait_ge(hu_ready, (n + 1) * FT)
                        act.activation(hu[:, 1, :], ring[:, 3, :], ACT.Copy).then_inc(hu_copied, 1)
                        for m in range(FT):
                            act.wait_ge(agg_ready, n * FT + m + 1)
                            act.activation(agg.hi[:, m, :], high[:, m, :], ACT.Copy).then_inc(agg_hi_ready, 1)
                    if not s.first:
                        for m in range(FT):
                            act.wait_ge(hv_ready, (n - 1) * FT + m + 1)
                            act.activation(hv[:, m, :], high[:, 2 + m, :], ACT.Tanh, bias=bias[:, 2, m:m + 1])\
                                .then_inc(hv_done, 1)
                    if s.enters is not None:
                        enter(s.enters, s.other)
                    for m in range(FT):
                        if not s.first:
                            act.wait_ge(h_done, (n - 1) * FT + m + 1)
                            if s.before_step < STEPS - 1:
                                act.activation(hp[s.other].hi[:, m, :], h[s.other][:, m, :], ACT.Copy)\
                                    .then_inc(h_hi_ready, 1)
                    for m in range(FT):
                        if not s.last:
                            act.wait_ge(r_added, n * FT + m + 1)
                            act.activation(r[:, m, :], r[:, m, :], ACT.Sigmoid, bias=bias[:, 1, m:m + 1])\
                                .then_inc(r_done, 1)

                enter(0, 0)
                halves(act, body)

            @block.vector
            def _(dve):
                dve.wait_ge(w_loaded, 16 * 5)
                dve.tensor_tensor(w_stage[:, :, :, 0:D], w_stage[:, :, :, 0:D], w_stage[:, :, :, D:2 * D], ALU.add)\
                    .then_inc(halves_added, 1)
                ln.dve_stats(dve, 0)
                ln.dve_normalise(dve, 0)
                dve.wait_ge(b_loaded, 16 * 5)
                for n, (wb, ub) in enumerate(((0, 3), (1, 3), (2, 4))):
                    dve.tensor_tensor(bias[:, n, :], b_stage[:, wb, :], b_stage[:, ub, :], ALU.add).then_inc(b_ready, 1)
                for n, m in enumerate(mats):
                    dve.wait_ge(wT_hi_ready, n + 1)
                    bank = ring[:, n, :] if n < 4 else high[:, 0, :]
                    dve.tensor_tensor(wT[m].lo[:], bank.rearrange("p (k o) -> p k o", k=FT), f32(wT[m].hi[:]),
                                      ALU.subtract).then_inc(wT_lo_ready, 1)
                dve.wait_ge(wT_hi_ready, 6)
                dve.tensor_tensor(adj.lo[:], adjT[:], f32(adj.hi[:]), ALU.subtract).then_inc(wT_lo_ready, 1)

                def enter(c, me):
                    for f in range(FT):
                        dve.wait_ge(h0_hi_ready, c * FT + f + 1)
                        dve.scalar_tensor_tensor(hp[me].lo[:, f, :], ring[:, 2 + f, :], 0.0,
                                                 f32(hp[me].hi[:, f, :]), ALU.max, ALU.subtract)\
                            .then_inc(h0_lo_ready, 1)

                def leave(c):
                    for q in range(2):
                        dve.wait_ge(final_ready, c * 2 + q + 1)
                        xc = x[:, bass.ds(c * CT + 2 * q, 2), :]
                        dve.tensor_tensor(xc, xc, ring[:, 2 + q, :].rearrange("p (t d) -> p t d", t=2),
                                          ALU.add).then_inc(x_done, 1)

                def body(s):
                    n = s.n
                    if s.left is not None:
                        leave(s.left)
                    if not s.last:
                        for q in range(2):
                            dve.wait_ge(tok_hi_ready, n * 2 + q + 1)
                            dve.tensor_tensor(tok.lo[:, 2 * q:2 * q + 2, :],
                                              ring[:, q, :].rearrange("p (t d) -> p t d", t=2),
                                              f32(tok.hi[:, 2 * q:2 * q + 2, :]), ALU.subtract)\
                                .then_inc(tok_lo_ready, 1)
                    old, new = s.h_before(), h[s.other]
                    if not s.first:
                        dve.wait_ge(r_done, n * FT)
                        dve.tensor_tensor(rh[:], r[:], old[:], ALU.mult).then_inc(rh_done, 1)
                        dve.wait_ge(rh_hi_ready, n)
                        dve.tensor_tensor(rhp.lo[:], rh[:], f32(rhp.hi[:]), ALU.subtract).then_inc(rh_lo_ready, 1)
                    if not s.last:
                        for m in range(FT):
                            dve.wait_ge(agg_hi_ready, n * FT + m + 1)
                            dve.tensor_tensor(agg.lo[:, m, :], high[:, m, :], f32(agg.hi[:, m, :]),
                                              ALU.subtract).then_inc(agg_lo_ready, 1)
                    if s.k == 1 and not s.stops:
                        ln.dve_stats(dve, s.chunk + 1)
                    if s.k == 2 and not s.stops:
                        ln.dve_normalise(dve, s.chunk + 2)
                    if s.k == 3 and not s.stops:
                        ln.dve_stats(dve, s.chunk + 2)
                    if not s.first:
                        dve.wait_ge(z_done, n * FT)
                        for m in range(FT):
                            dve.wait_ge(hv_done, (n - 1) * FT + m + 1)
                            dve.tensor_tensor(hv[:, m, :], hv[:, m, :], old[:, m, :], ALU.subtract)\
                                .then_inc(hv_minus_h, 1)
                            dve.wait_ge(hv_minus_h, (n - 1) * FT + m + 1)
                            dve.tensor_tensor(hv[:, m, :], hv[:, m, :], z[:, m, :], ALU.mult).then_inc(hv_gated, 1)
                            dve.wait_ge(hv_gated, (n - 1) * FT + m + 1)
                            dve.tensor_tensor(new[:, m, :], old[:, m, :], hv[:, m, :], ALU.add).then_inc(h_done, 1)
                    if not s.last:
                        dve.wait_ge(hu_copied, (n + 1) * FT)
                        for m in range(FT):
                            dve.wait_ge(r_ready, n * FT + m + 1)
                            dve.tensor_tensor(r[:, m, :], ring[:, m, :], hu[:, m, :], ALU.add).then_inc(r_added, 1)
                    if s.enters is not None:
                        enter(s.enters, s.other)
                    if not s.first and s.before_step < STEPS - 1:
                        for m in range(FT):
                            dve.wait_ge(h_hi_ready, (s.before_later - 1) * FT + m + 1)
                            dve.tensor_tensor(hp[s.other].lo[:, m, :], h[s.other][:, m, :],
                                              f32(hp[s.other].hi[:, m, :]), ALU.subtract).then_inc(h_lo_ready, 1)
                    if s.k == 5 and s.enters is not None:
                        ln.dve_normalise(dve, s.chunk + 2)
                    if not s.last:
                        for m in range(FT):
                            dve.wait_ge(z_ready, n * FT + m + 1)
                            dve.tensor_tensor(z[:, m, :], high[:, m, :], hu[:, m, :], ALU.add).then_inc(z_added, 1)
                    if s.k == 0 and s.leaves is not None:
                        leave(s.leaves)

                enter(0, 0)
                ln.dve_stats(dve, 1)
                ln.dve_normalise(dve, 1)
                halves(dve, body)

            @block.tensor
            def _(pe):
                def columns(parts_, m):
                    return [pair(parts_, slice(None), k, slice(m * P, (m + 1) * P)) for k in range(FT)]

                def moving(parts_):
                    return [pair(parts_, slice(None), k, slice(None)) for k in range(FT)]

                def enter(c):
                    for f in range(FT):
                        ln.pe_transpose(pe, c, f, ring[:, 2 + f, :])

                pe.wait_ge(halves_added, 1)
                for n, m in enumerate(mats):
                    bank = ring[:, n, :] if n < 4 else high[:, 0, :]
                    for k in range(FT):
                        for o in range(FT):
                            src = w_stage[:, n, o, k * P:(k + 1) * P] if n < 3 else u_stage[:, n - 3, o, k * P:(k + 1) * P]
                            last = pe.transpose(bank[:, k * D + o * P:k * D + (o + 1) * P], src, ident[:])
                    last.then_inc(wT_ready, 1)
                pe.wait_ge(wT_lo_ready, 6)

                def body(s):
                    n = s.n
                    if not s.last:
                        if s.step == 0:
                            pe.wait_ge(h0_hi_ready, (s.chunk + 1) * FT)
                        else:
                            pe.wait_ge(h_done, (n - 1) * FT)
                        if not s.first:
                            pe.wait_ge(r_added, n * FT)
                        for q in range(2):
                            for t in (2 * q, 2 * q + 1):
                                for f in range(FT):
                                    at = (t % 2) * D + f * P
                                    last = pe.transpose(ring[:, q, at:at + P],
                                                        s.h_me()[:, f, t * P:(t + 1) * P], ident[:])
                            last.then_inc(tok_ready, 1)
                        if s.step == 0:
                            pe.wait_ge(h0_lo_ready, (s.chunk + 1) * FT)
                        else:
                            pe.wait_ge(h_lo_ready, (s.later - 1) * FT)
                        if s.left is not None:
                            pe.wait_ge(x_done, (s.left + 1) * 2)
                        elif s.k == 1:
                            pe.wait_ge(tok_lo_ready, n * 2 + 1)
                        elif not s.first:
                            pe.wait_ge(hu_copied, n * FT)
                        for m in range(FT):
                            product(pe, ring[:, 2 + m, :], columns(wT["u3"], m), moving(hp[s.me])).then_inc(hu_ready, 1)
                        pe.wait_ge(tok_lo_ready, (n + 1) * 2)
                        if not s.first:
                            pe.wait_ge(z_added, n * FT)
                        for m in range(FT):
                            for t in range(CT):
                                last = product(pe, high[:, m, t * P:(t + 1) * P],
                                               [pair(tok, slice(None), t, slice(m * P, (m + 1) * P))],
                                               [(adj.hi[:], adj.lo[:])])
                            last.then_inc(agg_ready, 1)
                    if not s.first:
                        pe.wait_ge(rh_lo_ready, n)
                        for m in range(FT):
                            product(pe, high[:, 2 + m, :], columns(wT["u5"], m), moving(rhp), begins=False)\
                                .then_inc(hv_ready, 1)
                    if s.enters is not None:
                        pe.wait_ge(hu_copied, (n + 1) * FT)
                        enter(s.enters)
                    if not s.last:
                        pe.wait_ge(agg_lo_ready, (n + 1) * FT)
                        for m in range(FT):
                            product(pe, ring[:, m, :], columns(wT["w4"], m), moving(agg)).then_inc(r_ready, 1)
                        for m in range(FT):
                            product(pe, high[:, m, :], columns(wT["w3"], m), moving(agg)).then_inc(z_ready, 1)
                        if not s.first:
                            pe.wait_ge(hv_done, n * FT)
                        for m in range(FT):
                            product(pe, high[:, 2 + m, :], columns(wT["w5"], m), moving(agg), ends=False)
                    if s.leaves is not None:
                        pe.wait_ge(h_done, n * FT)
                        if s.enters is not None:
                            pe.wait_ge(h0_lo_ready, (s.enters + 1) * FT)
                        elif not s.last:
                            pe.wait_ge(hu_copied, (n + 1) * FT)
                        else:
                            pe.wait_ge(x_done, s.leaves * 2)
                        for q in range(2):
                            for t in (2 * q, 2 * q + 1):
                                for f in range(FT):
                                    at = (t % 2) * D + f * P
                                    last = pe.transpose(ring[:, 2 + q, at:at + P],
                                                        h[s.other][:, f, t * P:(t + 1) * P], ident[:])
                            last.then_inc(final_ready, 1)

                enter(0)
                halves(pe, body)


def build(nc, a, out):
    with ExitStack() as ctx:
        x = ctx.enter_context(nc.sbuf_tensor("x", [P, TILES, D], F32))
        ident = ctx.enter_context(nc.sbuf_tensor("ident", [P, P], F32))
        scores = ctx.enter_context(nc.psum_tensor("scores", [P, 4, BANK], F32))
        ring = ctx.enter_context(nc.psum_tensor("ring", [P, 4, BANK], F32))
        ident_steps = ctx.enter_context(nc.semaphore("ident_steps"))
        ctx.enter_context(nc.allow_non_contiguous_dma(reason="small transposed and replicated loads"))
        with nc.Block() as block:
            @block.gpsimd
            def _(pool):
                pool.memset(ident[:], 0.0).then_inc(ident_steps, 1)
                pool.wait_ge(ident_steps, 1)
                pool.affine_select(out=ident[:], in_=ident[:], compare_op=ALU.not_equal, fill=1.0, base=0,
                                   pattern=[[-1, P]], channel_multiplier=1).then_inc(ident_steps, 1)
                pool.wait_ge(ident_steps, 2)

        def rows(ap):
            return ap.rearrange("(k p) n -> p k n", p=P)

        adj = a["adj"]
        attention_phase(nc, "l0", x, ident, (scores, ring), dict(
            adj=adj, wq=rows(a["L0_gnn_Wq"]), wk=rows(a["L0_gnn_Wk"]), wv=rows(a["L0_gnn_Wv"]),
            wo=rows(a["L0_gnn_Wo"]), bq=a["L0_gnn_bq"], bk=a["L0_gnn_bk"], bv=a["L0_gnn_bv"],
            bo=a["L0_gnn_bo"], fill="additive"), first_load=a["x"])
        wqkv = rows(a["L1_gnn_w_qkv"])
        attention_phase(nc, "l1", x, ident, (scores, ring), dict(
            adj=adj, wq=wqkv[:, :, 0:D], wk=wqkv[:, :, D:2 * D], wv=wqkv[:, :, 2 * D:3 * D],
            wo=rows(a["L1_gnn_w_proj"]), bo=a["L1_gnn_b_proj"], fill="exclusive"),
            tail_norm=dict(gamma=a["L1_gnn_ln_gamma"], beta=a["L1_gnn_ln_beta"]))
        weights = RecurrenceWeights(nc, ctx, a)
        graph_attention_phase(nc, x, ident, (scores, ring), a, weights)
        recurrence_phase(nc, x, ident, (scores, ring), a, weights, out)


INPUTS = ["x", "adj", "L0_gnn_Wq", "L0_gnn_bq", "L0_gnn_Wk", "L0_gnn_bk", "L0_gnn_Wv", "L0_gnn_bv",
          "L0_gnn_Wo", "L0_gnn_bo", "L1_gnn_w_qkv", "L1_gnn_w_proj", "L1_gnn_b_proj", "L1_gnn_ln_gamma",
          "L1_gnn_ln_beta", "L2_gnn_W", "L2_gnn_a", "L2_gnn_beta", "L3_gnn_w3_w", "L3_gnn_w3_b",
          "L3_gnn_u3_w", "L3_gnn_u3_b", "L3_gnn_w4_w", "L3_gnn_w4_b", "L3_gnn_w5_w", "L3_gnn_w5_b",
          "L3_gnn_u5_w", "L3_gnn_u5_b"]


def kernel(**inputs):
    import numpy as np
    import concourse.bacc as bacc
    from concourse import mybir as mb
    from concourse.bass_utils import run_bass_kernel_spmd as run

    nc = bacc.Bacc("TRN2", target_bir_lowering=False, num_devices=1)
    arrays, handles = {}, {}
    for name in INPUTS:
        v = np.ascontiguousarray(inputs[name])
        arrays[f"in_{name}"] = v
        handles[name] = nc.dram_tensor(f"in_{name}", v.shape, mb.dt.from_np(v.dtype), kind="ExternalInput").ap()
    out = nc.dram_tensor("out_x", (B, N, D), mb.dt.float32, kind="ExternalOutput").ap()
    build(nc, handles, out)
    result = run(nc, [arrays], core_ids=[0])
    return result.results[0]["out_x"]
```
